# Optimizing a Trainium2 kernel written in Bass

```python
import numpy as np
import jax
import jax.numpy as jnp

def _softmax(x, axis=-1):
    return jax.nn.softmax(x, axis=axis)
def _gelu(x):
    return jax.nn.gelu(x, approximate=True)
def _silu(x):
    return jax.nn.silu(x)
def _sigmoid(x):
    return jax.nn.sigmoid(x)
def _layernorm(x, axis=-1, eps=1e-5):
    m = jnp.mean(x, axis=axis, keepdims=True)
    v = jnp.var(x, axis=axis, keepdims=True)
    return (x - m) / jnp.sqrt(v + eps)
def _scatter_add(tgt, idx, src, axis=0):
    return tgt.at[idx].add(src)
def _segment_sum(src, seg, n):
    return jax.ops.segment_sum(src, seg, n)

kernel_name = 'mk_audio_tower_d1_tok_audfeat256_c0a4a2'

def setup_inputs(seed: int = 0):
    np.random.seed(seed)
    _w = jnp.asarray
    def _rec_inputs():
        import jax
        import jax.numpy as jnp
        _rk = jax.random.key(seed)
        x = (-0.000392918 + 0.999932 * jax.random.normal(jax.random.fold_in(_rk, 1), (128, 1000, 16), jnp.float32))
        return x
    x = _rec_inputs()
    def _L0_tok_setup():
        import jax, jax.numpy as jnp
        import numpy as np
        PATCH = 16
        STRIDE = 8
        EPS = 1e-05
        key = jax.random.key(seed)
        k1, k2, k3 = jax.random.split(key, 3)
        B, S, F, D = (128, 8192, 16, 256)
        in_dim = F * PATCH
        x = jax.random.normal(k1, (B, S, F), dtype=jnp.float32)
        bound = 1.0 / np.sqrt(in_dim)
        W = jax.random.uniform(k2, (D, in_dim), minval=-bound, maxval=bound, dtype=jnp.float32)
        b = jax.random.uniform(k3, (D,), minval=-bound, maxval=bound, dtype=jnp.float32)
        gamma = jnp.ones((D,), dtype=jnp.float32)
        beta = jnp.zeros((D,), dtype=jnp.float32)
        return {'x': x, 'W': W, 'b': b, 'gamma': gamma, 'beta': beta}
    _L0_tok_all = _L0_tok_setup()
    _L0_tok_in = {k: v for k, v in _L0_tok_all.items() if k in ('W', 'b', 'gamma', 'beta', )}
    del _L0_tok_all

    def _L0_attn_setup():
        import jax, jax.numpy as jnp
        import numpy as np
        B, N, D = (4, 4096, 256)
        key = jax.random.key(seed)
        ks = jax.random.split(key, 7)

        def xavier(k, shape):
            fan_in, fan_out = (shape[1], shape[0])
            a = jnp.sqrt(6.0 / (fan_in + fan_out))
            return jax.random.uniform(k, shape, jnp.float32, -a, a)
        return {'x': jax.random.normal(ks[0], (B, N, D), jnp.float32), 'Wq': xavier(ks[1], (D, D)), 'bq': jnp.zeros((D,), jnp.float32), 'Wk': xavier(ks[2], (D, D)), 'bk': jnp.zeros((D,), jnp.float32), 'Wv': xavier(ks[3], (D, D)), 'bv': jnp.zeros((D,), jnp.float32), 'scale': jnp.asarray([jnp.sqrt(jnp.float32(D))])}
    _L0_attn_all = _L0_attn_setup()
    _L0_attn_in = {k: v for k, v in _L0_attn_all.items() if k in ('Wq', 'bq', 'Wk', 'bk', 'Wv', 'bv', 'scale', )}
    del _L0_attn_all

    def _L0_ffn_setup():
        import jax, jax.numpy as jnp
        import numpy as np
        E, D, H, TOP_K = (6, 256, 256, 2)
        ROUTER_H = D // 2
        key = jax.random.key(seed)
        ks = jax.random.split(key, 12)
        s = 1.0 / np.sqrt(D)
        sh = 1.0 / np.sqrt(H)
        sr = 1.0 / np.sqrt(ROUTER_H)
        return {'features': jax.random.normal(ks[0], (8, 4096, D), dtype=jnp.float32), 'router_w1': jax.random.uniform(ks[1], (D, ROUTER_H), jnp.float32, -s, s), 'router_b1': jnp.zeros((ROUTER_H,), jnp.float32), 'router_w2': jax.random.uniform(ks[2], (ROUTER_H, E), jnp.float32, -sr, sr), 'router_b2': jnp.zeros((E,), jnp.float32), 'expert_w1': jax.random.uniform(ks[3], (E, D, H), jnp.float32, -s, s), 'expert_b1': jnp.zeros((E, H), jnp.float32), 'expert_w2': jax.random.uniform(ks[4], (E, H, H), jnp.float32, -sh, sh), 'expert_b2': jnp.zeros((E, H), jnp.float32), 'expert_w3': jax.random.uniform(ks[5], (E, H, D), jnp.float32, -sh, sh), 'expert_b3': jnp.zeros((E, D), jnp.float32)}
    _L0_ffn_all = _L0_ffn_setup()
    _L0_ffn_in = {k: v for k, v in _L0_ffn_all.items() if k in ('router_w1', 'router_b1', 'router_w2', 'router_b2', 'expert_w1', 'expert_b1', 'expert_w2', 'expert_b2', 'expert_w3', 'expert_b3', )}
    del _L0_ffn_all

    return {
        "x": x,
        "L0_tok_W": _L0_tok_in["W"],
        "L0_tok_b": _L0_tok_in["b"],
        "L0_tok_gamma": _L0_tok_in["gamma"],
        "L0_tok_beta": _L0_tok_in["beta"],
        "L0_attn_Wq": _L0_attn_in["Wq"],
        "L0_attn_bq": _L0_attn_in["bq"],
        "L0_attn_Wk": _L0_attn_in["Wk"],
        "L0_attn_bk": _L0_attn_in["bk"],
        "L0_attn_Wv": _L0_attn_in["Wv"],
        "L0_attn_bv": _L0_attn_in["bv"],
        "L0_attn_scale": _L0_attn_in["scale"],
        "L0_ffn_router_w1": _L0_ffn_in["router_w1"],
        "L0_ffn_router_b1": _L0_ffn_in["router_b1"],
        "L0_ffn_router_w2": _L0_ffn_in["router_w2"],
        "L0_ffn_router_b2": _L0_ffn_in["router_b2"],
        "L0_ffn_expert_w1": _L0_ffn_in["expert_w1"],
        "L0_ffn_expert_b1": _L0_ffn_in["expert_b1"],
        "L0_ffn_expert_w2": _L0_ffn_in["expert_w2"],
        "L0_ffn_expert_b2": _L0_ffn_in["expert_b2"],
        "L0_ffn_expert_w3": _L0_ffn_in["expert_w3"],
        "L0_ffn_expert_b3": _L0_ffn_in["expert_b3"],
    }

def reference(x, L0_tok_W, L0_tok_b, L0_tok_gamma, L0_tok_beta, L0_attn_Wq, L0_attn_bq, L0_attn_Wk, L0_attn_bk, L0_attn_Wv, L0_attn_bv, L0_attn_scale, L0_ffn_router_w1, L0_ffn_router_b1, L0_ffn_router_w2, L0_ffn_router_b2, L0_ffn_expert_w1, L0_ffn_expert_b1, L0_ffn_expert_w2, L0_ffn_expert_b2, L0_ffn_expert_w3, L0_ffn_expert_b3):
    import jax
    import jax.numpy as jnp
    def _L0_tok_ref(x, W, b, gamma, beta):
        import jax, jax.numpy as jnp
        import numpy as np
        PATCH = 16
        STRIDE = 8
        EPS = 1e-05
        B, S, F = x.shape
        starts = jnp.arange(0, S - PATCH + 1, STRIDE)
        idx = starts[:, None] + jnp.arange(PATCH)[None, :]
        patches = x[:, idx, :].reshape(B, idx.shape[0], PATCH * F)
        y = jnp.einsum('bpi,di->bpd', patches, W) + b
        mu = jnp.mean(y, axis=-1, keepdims=True)
        var = jnp.mean(jnp.square(y - mu), axis=-1, keepdims=True)
        return (y - mu) * jax.lax.rsqrt(var + EPS) * gamma + beta

    def _L0_attn_ref(x, Wq, bq, Wk, bk, Wv, bv, scale):
        import jax, jax.numpy as jnp
        import numpy as np
        B, N, D = (4, 4096, 256)
        q = jnp.einsum('bnd,ed->bne', x, Wq) + bq
        k = jnp.einsum('bnd,ed->bne', x, Wk) + bk
        v = jnp.einsum('bnd,ed->bne', x, Wv) + bv
        scores = jnp.einsum('bqd,bkd->bqk', q, k) / scale[0]
        attn = jax.nn.softmax(scores, axis=-1)
        out = jnp.einsum('bqk,bkd->bqd', attn, v)
        return out

    def _L0_ffn_ref(features, router_w1, router_b1, router_w2, router_b2, expert_w1, expert_b1, expert_w2, expert_b2, expert_w3, expert_b3):
        import jax, jax.numpy as jnp
        import numpy as np
        E, D, H, TOP_K = (6, 256, 256, 2)
        ROUTER_H = D // 2
        rh = jax.nn.relu(features @ router_w1 + router_b1)
        expert_logits = jax.nn.softmax(rh @ router_w2 + router_b2, axis=-1)
        top_w, top_i = jax.lax.top_k(expert_logits, TOP_K)
        routing_weights = jax.nn.softmax(top_w, axis=-1)
        h1 = jax.nn.relu(jnp.einsum('bsd,edh->bseh', features, expert_w1) + expert_b1)
        h2 = jax.nn.relu(jnp.einsum('bseh,ehf->bsef', h1, expert_w2) + expert_b2)
        expert_out = jnp.einsum('bsef,efo->bseo', h2, expert_w3) + expert_b3
        sel = jnp.take_along_axis(expert_out, top_i[:, :, :, None], axis=2)
        combined = jnp.sum(sel * routing_weights[..., None], axis=2)
        return combined

    h = _L0_tok_ref(x, L0_tok_W, L0_tok_b, L0_tok_gamma, L0_tok_beta)
    h = h + _L0_attn_ref(_layernorm(h, axis=-1), L0_attn_Wq, L0_attn_bq, L0_attn_Wk, L0_attn_bk, L0_attn_Wv, L0_attn_bv, L0_attn_scale)
    h = h + _L0_ffn_ref(_layernorm(h, axis=-1), L0_ffn_router_w1, L0_ffn_router_b1, L0_ffn_router_w2, L0_ffn_router_b2, L0_ffn_expert_w1, L0_ffn_expert_b1, L0_ffn_expert_w2, L0_ffn_expert_b2, L0_ffn_expert_w3, L0_ffn_expert_b3)
    return h


_drawn_inputs = setup_inputs


def setup_inputs(seed=0):
    import zlib

    import numpy as np

    out = dict(_drawn_inputs(seed))
    spreads = {'L0_tok_gamma': (1.0, 0.2),
     'L0_tok_beta': (0.0, 0.1),
     'L0_attn_bq': (0.0, 0.457),
     'L0_attn_bk': (0.0, 0.8),
     'L0_attn_bv': (0.0, 0.1),
     'L0_ffn_router_b1': (0.0, 0.1),
     'L0_ffn_router_b2': (0.0, 0.1),
     'L0_ffn_expert_b1': (0.0, 0.722),
     'L0_ffn_expert_b2': (0.0, 0.31),
     'L0_ffn_expert_b3': (0.0, 0.1)}
    factors = {}
    for name, (base, spread) in spreads.items():
        noise = np.random.default_rng([zlib.crc32(name.encode()), seed]).standard_normal(out[name].shape)
        drawn = base * np.exp(spread * noise) if base else spread * noise
        out[name] = jnp.asarray(drawn.astype(out[name].dtype))
    for name, factor in factors.items():
        out[name] = (out[name] * factor).astype(out[name].dtype)
    return out
```

```python
from contextlib import ExitStack

import numpy as np

import concourse.bass as bass
from concourse import mybir

F32 = mybir.dt.float32
F32R = mybir.dt.float32r
BF16 = mybir.dt.bfloat16
I32 = mybir.dt.int32
U32 = mybir.dt.uint32
ALU = mybir.AluOpType
ACT = mybir.ActivationFunctionType
AX_X = mybir.AxisListType.X

P = 128
BATCH, SEQ, FEAT = 128, 1000, 16
PATCH, STRIDE = 16, 8
TOK = (SEQ - PATCH) // STRIDE + 1
ROWS_X = SEQ * FEAT // P
D = 256
DC = D // P
NE, TOPK = 6, 2
E8 = 8
EPS = 1e-5
GB = 4
G = BATCH // GB
GT = GB * TOK
NTOK = BATCH * TOK
DEPTH = 5
RING = 3

TILE = 512
TB = TILE // P
REGION = NTOK + TILE
NT = (NTOK * TOPK + NE * (TILE - 1)) // TILE
REC = D + E8 + 1
SLOTS = 4
SMALL = 2 * DC + D + E8

LN1_N, AV_N, TOPK_N, POS_N = 29, 14, 25, 4


def wait(eng, sem, value):
    if isinstance(value, int) and value <= 0:
        return
    eng.wait_ge(sem, value)


def wait_apart(eng, sem, value, passed):
    eng.wait_ge(sem, value)
    eng.sem_inc(passed, 1)


def audio_tower(nc, x, tok_w, tok_b, tok_gamma, tok_beta, wq, bq, wk, bk, wv, bv, scale,
                rw1, rb1, rw2, rb2, ew1, ew2, ew3, esmall, out):
    with ExitStack() as ctx:
        def sb(name, shape, dt=F32):
            return ctx.enter_context(nc.sbuf_tensor(name, shape, dt))

        def sem(name):
            return ctx.enter_context(nc.semaphore(name))

        banks = [ctx.enter_context(nc.psum_tensor(f"bank{i}", [P, 512], F32)) for i in range(8)]

        rows_dram = nc.dram_tensor("expert_rows", [NE * REGION + TILE, REC], F32, kind="Internal").ap()
        acc_dram = nc.dram_tensor("residual", [NTOK + TILE, D], F32, kind="Internal").ap()
        split_dram = nc.dram_tensor("split_weights", [NE, P, 3 * 2 * DC * D], F32, kind="Internal").ap()

        ident = sb("ident", [P, P])
        before = sb("before", [P, P], BF16)
        ones = sb("ones", [P, P], BF16)
        tokw_sb = sb("tokw_sb", [P, DC, D])
        wq_sb, wk_sb, wv_sb = (sb(n, [P, DC, D]) for n in ("wq_sb", "wk_sb", "wv_sb"))
        rw1_sb = sb("rw1_sb", [P, DC, P])
        rw2_sb = sb("rw2_sb", [P, NE])
        tokb_bc, gamma_bc, beta_bc, bv_bc = (sb(n, [P, D]) for n in ("tokb_bc", "gamma_bc", "beta_bc", "bv_bc"))
        bq_raw, bk_col, bq_col = (sb(n, [P, DC]) for n in ("bq_raw", "bk_col", "bq_col"))
        rb1_col, scale_col, invs_col = (sb(n, [P, 1]) for n in ("rb1_col", "scale_col", "invs_col"))
        rb2_bc = sb("rb2_bc", [P, NE])
        iota8 = sb("iota8", [P, E8])
        neghalf = sb("neghalf", [P, GB])
        tokid = sb("tokid", [P, GB])
        pad_rows = sb("pad_rows", [P, TB, REC])

        x_in = sb("x_in", [P, RING, GB, P])
        xT = sb("xT", [P, GB * ROWS_X])
        y = sb("y", [P, GB, D])
        h = sb("h", [P, RING, GB, D])
        xn1 = sb("xn1", [P, GB, D])
        xn1T = sb("xn1T", [P, DC, GT])
        qT, kT = sb("qT", [P, DC, GT]), sb("kT", [P, DC, GT])
        v_sb = sb("v_sb", [P, GB, D])
        probs = sb("probs", [P, GB, TOK])
        pT = sb("pT", [P, GB * TOK])
        xn2T = sb("xn2T", [P, DC, GT])
        rhT = sb("rhT", [P, GT])
        rec = sb("rec", [P, RING, GB, REC])
        stats = sb("stats", [P, 3, GB, 6])
        mv = sb("mv", [P, 3, GB, 2])
        vareps = sb("vareps", [P, 3, GB])
        rstd = sb("rstd", [P, 3, GB])
        nmr = sb("nmr", [P, 2, GB])
        negmax, rowsum, rinv = sb("negmax", [P, GB]), sb("rowsum", [P, GB]), sb("rinv", [P, GB])
        logits, lshift, pexp, pn, mx = (sb(n, [P, GB, E8]) for n in ("logits", "lshift", "pexp", "pn", "mx"))
        lmax, psums, pinv = (sb(n, [P, GB]) for n in ("lmax", "psums", "pinv"))
        mxi = sb("mxi", [P, GB, E8], U32)
        gap, gexp, gden = (sb(n, [P, GB]) for n in ("gap", "gexp", "gden"))
        gate2 = sb("gate2", [P, GB, TOPK])
        choice = sb("choice", [P, GB, TOPK])
        onehot = sb("onehot", [P, GB, TOPK, E8])
        gated = sb("gated", [P, GB, TOPK, E8])
        picked = sb("picked", [P, GB * E8], BF16)
        place = sb("place", [P, RING, GB + 1, E8])
        placed = sb("placed", [P, GB, TOPK, E8])
        rowf = sb("rowf", [P, GB, TOPK])
        row_i = sb("row_i", [P, RING, GB, TOPK], I32)

        t_iota = sb("t_iota", [1, NT])
        t_base = sb("t_base", [1, E8])
        t_i = sb("t_i", [1, E8], I32)
        t_ti = sb("t_ti", [1, E8], I32)
        t_nt, t_cum, t_delta = sb("t_nt", [1, E8]), sb("t_cum", [1, E8]), sb("t_delta", [1, E8])
        t_zero = sb("t_zero", [1, E8])
        t_ge, t_prod = sb("t_ge", [1, NT, E8]), sb("t_prod", [1, NT, E8])
        t_row, t_exp, t_load = sb("t_row", [1, NT]), sb("t_exp", [1, NT]), sb("t_load", [1, NT])
        pad_at = sb("pad_at", [1, E8], I32)
        row_tab, exp_tab, load_tab = (sb(n, [1, NT], I32) for n in ("row_tab", "exp_tab", "load_tab"))

        w_sb = [sb(f"w_sb{i}", [P, 3, 2, DC, D], F32R) for i in range(SLOTS)]
        small = sb("small", [P, SLOTS, SMALL])
        xg = sb("xg", [P, SLOTS, TB, REC])
        xv = sb("xv", [P, DC, TILE])
        x_hi, x_lo = sb("x_hi", [P, DC, TILE], F32R), sb("x_lo", [P, DC, TILE], F32R)
        h1v = sb("h1v", [P, DC, TILE])
        h1_hi, h1_lo = sb("h1_hi", [P, DC, TILE], F32R), sb("h1_lo", [P, DC, TILE], F32R)
        h2v = sb("h2v", [P, DC, TILE])
        h2_hi, h2_lo = sb("h2_hi", [P, DC, TILE], F32R), sb("h2_lo", [P, DC, TILE], F32R)
        yo = sb("yo", [P, 2, TB, D])
        gsel = sb("gsel", [P, TB, E8])
        gcol = sb("gcol", [P, 2, TB])

        S = {n: sem(n) for n in (
            "const_loaded", "pool_const", "dve_const", "invs", "raw_w0", "raw_w1", "w_high", "w_low",
            "w_stored0", "w_stored1", "dummy_cleared",
            "xT_ps", "xT_sb", "tok_ps", "ln1", "rstd1", "rstd2", "rstd3", "xn1_ready", "xn1T_ps", "xn1T_sb",
            "qk_ps", "qk_sb", "v_ps", "v_ready", "scores_ps", "score_max", "probs_ready", "pT_ps", "pT_sb",
            "av_ps", "av", "xn2_ready", "xn2T_ps", "xn2T_sb", "rh_ps", "rh_sb", "logits_ps", "topk", "gate_exp",
            "pos_ps", "pos", "table", "pads_written", "routed",
            "txT_ps", "tx_act", "tx_lo", "h1_ps", "h1_v", "h1_split", "h2_ps", "h2_v", "h2_split",
            "y_ps", "y_dve", "y_gated", "y_added", "copied", "dve_passed", "pool_passed")}
        x_loaded = [sem(f"x_loaded{i}") for i in range(RING)]
        h2_stored = [sem(f"h2_stored{i}") for i in range(RING)]
        scattered = [sem(f"scattered{i}") for i in range(RING)]
        tile_loaded = [sem(f"tile_loaded{i}") for i in range(SLOTS)]

        N_CONST = 16 * 15

        def uses(slot):
            return (G - slot + RING - 1) // RING

        def pipeline(eng, step, first=0):
            def straight(it):
                def group_of(s):
                    g = it - s
                    return (g, g % RING, g // RING) if 0 <= g < G else None
                step(it, group_of)

            rounds = (G - DEPTH + 1) // RING
            for it in range(DEPTH - 1):
                straight(it)
            with eng.Fori(0, rounds) as k:
                for u in range(RING):
                    c0 = DEPTH - 1 + u

                    def group_of(s, c0=c0):
                        c = c0 - s
                        return k * RING + c, c % RING, k + c // RING
                    step(k * RING + c0, group_of)
            for it in range(DEPTH - 1 + rounds * RING, G + DEPTH - 1):
                straight(it)

        def bank_read(eng, *uses):
            for s, g, count in uses:
                if not isinstance(g, int) or 0 <= g < G:
                    eng.wait_ge(s, count)
                    return

        def tiles(eng, step):
            head = SLOTS + 1
            rounds = (NT - head) // SLOTS
            for t in range(head):
                step(t, t % SLOTS, t // SLOTS)
            with eng.Fori(0, rounds) as k:
                for u in range(SLOTS):
                    step(k * SLOTS + head + u, (head + u) % SLOTS, k + (head + u) // SLOTS)
            for t in range(head + rounds * SLOTS, NT + 1):
                step(t, t % SLOTS, t // SLOTS)

        block = ctx.enter_context(nc.Block())

        def store_split(sp, n):
            e, layer, slot = n // 3, n % 3, n % 2
            sp.wait_ge(S["w_high"], n + 1)
            sp.wait_ge(S["w_low"], n + 1)
            sp.dma_start(split_dram[e].rearrange("p (l n) -> p l n", l=3)[:, layer, :],
                         w_sb[slot][:, 0, :, :, :].rearrange("p b c n -> p (b c n)").bitcast(F32)
                         ).then_inc(S[f"w_stored{slot}"], 16)

        @block.sync
        def _(sp):
            def const(dst, src):
                sp.dma_start(dst, src).then_inc(S["const_loaded"], 16)

            for dst, src in ((tokw_sb, tok_w), (wq_sb, wq), (wk_sb, wk), (wv_sb, wv), (rw1_sb, rw1)):
                const(dst[:], src.rearrange("(c p) n -> p c n", p=P))
            const(rw2_sb[:], rw2)
            for dst, src in ((tokb_bc, tok_b), (gamma_bc, tok_gamma), (beta_bc, tok_beta), (bv_bc, bv), (rb2_bc, rb2)):
                const(dst[:], src.to_broadcast([P, src.shape[1]]))
            const(bq_raw[:], bq)
            const(bk_col[:], bk)
            const(rb1_col[:], rb1)
            const(scale_col[:], scale.to_broadcast([P, 1]))

            raw = [w_sb[2], w_sb[3]]
            for e in range(NE):
                for layer, w in enumerate((ew1, ew2, ew3)):
                    n = e * 3 + layer
                    stage = xg[:, n % 2, :, 0:D]
                    if n >= 2:
                        sp.wait_ge(S["w_low"], n - 1)
                    sp.dma_start(stage[:, 0:DC, :], w[e].rearrange("(c p) n -> p c n", p=P)).then_inc(
                        S[f"raw_w{n % 2}"], 16)
                    if n >= 1:
                        store_split(sp, n - 1)
            store_split(sp, NE * 3 - 1)
            sp.wait_ge(S["pool_const"], 8)
            sp.dma_start(acc_dram[NTOK:NTOK + TILE, :].rearrange("(p j) n -> p j n", p=P),
                         pad_rows[:, :, 0:D]).then_inc(S["dummy_cleared"], 16)

            def load_x(g, slot):
                wait(sp, S["xT_ps"], g - RING + 1)
                sp.dma_start(x_in[0:ROWS_X, slot, :, :],
                             x[bass.ds(g * GB, GB), :, :].rearrange("b r n -> r b n")).then_inc(x_loaded[slot], 16)

            load_x(0, 0)

            def step(it, group_of):
                if not isinstance(it, int) or it + 1 < G:
                    load_x(it + 1, ((group_of(0) or (0, it % RING))[1] + 1) % RING)
                if group_of(2):
                    g, slot, rnd = group_of(2)
                    sp.wait_ge(S["av"], g * AV_N + 1 + GB)
                    sp.dma_start(acc_dram[bass.ds(g * GT, GT), :].rearrange("(b p) n -> p b n", p=TOK),
                                 h[0:TOK, slot, :, :]).then_inc(h2_stored[slot], 16)

            pipeline(sp, step)

            sp.wait_ge(S["table"], 14)
            for i in range(RING):
                sp.wait_ge(scattered[i], 16 * GB * TOPK * uses(i))
                sp.wait_ge(h2_stored[i], 16 * uses(i))
            sp.wait_ge(S["dummy_cleared"], 16)
            sp.wait_ge(S["w_stored0"], 16 * 9)
            sp.wait_ge(S["w_stored1"], 16 * 9)
            for e in range(NE):
                at = sp.value_load(pad_at[0:1, e:e + 1], min_val=0, max_val=NE * REGION)
                sp.dma_start(rows_dram[bass.ds(at, TILE), :].rearrange("(p j) n -> p (j n)", p=P),
                             pad_rows[:].rearrange("p j n -> p (j n)")).then_inc(S["pads_written"], 16)
            sp.dma_start(rows_dram[NE * REGION:NE * REGION + TILE, :].rearrange("(p j) n -> p (j n)", p=P),
                         pad_rows[:].rearrange("p j n -> p (j n)")).then_inc(S["pads_written"], 16)
            sp.wait_ge(S["pads_written"], 16 * (NE + 1))
            sp.sem_inc(S["routed"], 1)

            def load_tile(t, slot, rnd):
                if isinstance(t, int) and t >= NT:
                    return
                wait(sp, S["y_added"], (t - SLOTS + 1) * 16 * TB)
                row = sp.value_load(row_tab[0:1, bass.ds(t, 1)], min_val=0, max_val=NE * REGION)
                expert = sp.value_load(exp_tab[0:1, bass.ds(t, 1)], min_val=0, max_val=NE - 1)
                fresh = sp.value_load(load_tab[0:1, bass.ds(t, 1)], min_val=0, max_val=1)
                sp.dma_start(xg[:, slot, :, :].rearrange("p j n -> p (j n)"),
                             rows_dram[bass.ds(row, TILE), :].rearrange("(p j) n -> p (j n)", p=P)
                             ).then_inc(tile_loaded[slot], 16)
                sp.dma_start(w_sb[slot][:].rearrange("p a b c n -> p (a b c n)").bitcast(F32),
                             split_dram[bass.ds(expert, 1), :, :].rearrange("o p n -> (o p) n"),
                             cond=fresh != 0).then_inc(tile_loaded[slot], 16)
                sp.dma_start(small[:, slot, :], esmall[bass.ds(expert, 1), :, :].rearrange("o p n -> (o p) n")
                             ).then_inc(tile_loaded[slot], 16)

            tiles(sp, load_tile)

            sp.wait_ge(S["y_added"], NT * 16 * TB)
            for q in range(4):
                a, b = q * NTOK // 4, (q + 1) * NTOK // 4
                sp.dma_start(out[a:b, :].rearrange("(p j) n -> p (j n)", p=P),
                             acc_dram[a:b, :].rearrange("(p j) n -> p (j n)", p=P)).then_inc(S["copied"], 16)
            sp.wait_ge(S["copied"], 64)

        @block.gpsimd
        def _(pool):
            done = S["pool_const"]
            pool.memset(ident[:], 0.0).then_inc(done, 1)
            pool.memset(before[:], 0.0).then_inc(done, 1)
            pool.memset(ones[:], 1.0).then_inc(done, 1)
            pool.memset(pad_rows[:], 0.0).then_inc(done, 1)
            pool.wait_ge(done, 4)
            pool.affine_select(out=ident[:], in_=ident[:], compare_op=ALU.not_equal, fill=1.0, base=0,
                               pattern=[[-1, P]], channel_multiplier=1).then_inc(done, 1)
            pool.affine_select(out=before[:], in_=before[:], compare_op=ALU.is_ge, fill=1.0, base=0,
                               pattern=[[-1, P]], channel_multiplier=1).then_inc(done, 1)
            pool.iota(pad_rows[:, :, D + E8:REC].bitcast(I32).rearrange("p j o -> p (j o)"), [[1, TB]], base=NTOK,
                      channel_multiplier=TB).then_inc(done, 1)
            pool.memset(neghalf[:], -0.5).then_inc(done, 1)
            pool.iota(iota8[:], [[1, E8]], base=0, channel_multiplier=0,
                      allow_small_or_imprecise_dtypes=True).then_inc(done, 1)
            pool.iota(tokid[:], [[TOK, GB]], base=0, channel_multiplier=1,
                      allow_small_or_imprecise_dtypes=True).then_inc(done, 1)
            pool.iota(place[:, RING - 1, GB, :], [[REGION, E8]], base=0, channel_multiplier=0,
                      allow_small_or_imprecise_dtypes=True).then_inc(done, 1)
            pool.iota(t_iota[:], [[1, NT]], base=0, channel_multiplier=0,
                      allow_small_or_imprecise_dtypes=True).then_inc(done, 1)
            pool.iota(t_base[:], [[REGION, E8]], base=0, channel_multiplier=0,
                      allow_small_or_imprecise_dtypes=True).then_inc(done, 1)
            pool.memset(t_zero[:], 0.0).then_inc(done, 1)
            pool.memset(logits[:], -1e30).then_inc(done, 1)

            def inverse_std(which, ready, g):
                pool.tensor_scalar(vareps[0:TOK, which, :], mv[0:TOK, which, :, 1], EPS, None,
                                   ALU.add).then_inc(ready, 1)
                pool.wait_ge(ready, g * 2 + 1)
                pool.tensor_tensor(rstd[0:TOK, which, :], vareps[0:TOK, which, :], neghalf[0:TOK, :],
                                   ALU.pow).then_inc(ready, 1)

            def step(it, group_of):
                if group_of(0):
                    g, slot, rnd = group_of(0)
                    wait_apart(pool, S["ln1"], g * LN1_N + 3 * GB, S["pool_passed"])
                    inverse_std(0, S["rstd1"], g)
                    wait(pool, S["xn1_ready"], g * GB)
                    wait_apart(pool, S["ln1"], g * LN1_N + 7 * GB, S["pool_passed"])
                    inverse_std(1, S["rstd2"], g)
                if group_of(2):
                    g, slot, rnd = group_of(2)
                    wait(pool, S["xn2_ready"], g * GB)
                    wait_apart(pool, S["av"], g * AV_N + 1 + 3 * GB, S["pool_passed"])
                    inverse_std(2, S["rstd3"], g)
                if group_of(4):
                    g, slot, rnd = group_of(4)
                    pool.wait_ge(S["pos"], (g + 1) * POS_N)
                    pool.wait_ge(S["topk"], (g + 1) * TOPK_N)
                    wait_apart(pool, S["xn2_ready"], (g + 1) * GB, S["pool_passed"])
                    for j in range(GB):
                        for k in range(TOPK):
                            pool.indirect_dma_start(
                                rows_dram, bass.IndirectOffsetOnAxis(ap=row_i[0:TOK, slot, j, k:k + 1], axis=0),
                                rec[0:TOK, slot, j, :], None).then_inc(scattered[slot], 16)

            pipeline(pool, step)

            pool.wait_ge(S["routed"], 1)

            def add_tile(t, slot, rnd):
                if isinstance(t, int) and t == 0:
                    return
                s = (slot - 1) % SLOTS
                ys = (slot - 1) % 2
                wait(pool, S["y_added"], (t - 1) * 16 * TB)
                wait_apart(pool, S["y_gated"], t * TB, S["pool_passed"])
                for j in range(TB):
                    pool.indirect_dma_start(
                        acc_dram, bass.IndirectOffsetOnAxis(ap=xg[:, s, j, D + E8:REC].bitcast(I32), axis=0),
                        yo[:, ys, j, :], None, compute_op=ALU.add).then_inc(S["y_added"], 16)

            tiles(pool, add_tile)

        @block.tensor
        def _(pe):
            pe.wait_ge(S["const_loaded"], N_CONST)
            pe.wait_ge(S["pool_const"], 6)

            def step(it, group_of):
                x0, x1, x2, x3, x4 = (group_of(s) for s in range(DEPTH))
                if x0:
                    g, slot, rnd = x0
                    pe.wait_ge(x_loaded[slot], rnd * 16 + 16)
                    bank_read(pe, (S["topk"], it - 4, (it - 4) * TOPK_N + 1), (S["qk_sb"], it - 2, (it - 2) * 4 + 1),
                              (S["xT_sb"], it - 1, it))
                    for j in range(GB):
                        mm = pe.transpose(banks[0][:, j * ROWS_X:(j + 1) * ROWS_X],
                                          x_in[0:ROWS_X, slot, j, :], ident[0:ROWS_X, 0:ROWS_X])
                    mm.then_inc(S["xT_ps"], 1)
                if x1:
                    g, slot, rnd = x1
                    for c in range(DC):
                        bank_read(pe, (S["av"], it - 3, (it - 3) * AV_N + 3 + 2 * c),
                                  (S["qk_sb"], it - 2, (it - 2) * 4 + 2 + c))
                        for j in range(GB):
                            pe.wait_ge(S["xn1_ready"], g * GB + j + 1)
                            mm = pe.transpose(banks[1 + c][:, j * TOK:(j + 1) * TOK],
                                              xn1[0:TOK, j, c * P:(c + 1) * P], ident[0:TOK, 0:TOK])
                        mm.then_inc(S["xn1T_ps"], 1)
                if x3:
                    g, slot, rnd = x3
                    for c in range(DC):
                        if c == 0:
                            bank_read(pe, (S["qk_sb"], it - 2, (it - 2) * 4 + 4), (S["xn2T_sb"], it - 4, (it - 4) * 2 + 1))
                        else:
                            bank_read(pe, (S["pT_sb"], it - 3, it - 2), (S["pos"], it - 5, (it - 5) * POS_N + 1),
                                      (S["xn2T_sb"], it - 4, (it - 4) * 2 + 2))
                        for j in range(GB):
                            pe.wait_ge(S["xn2_ready"], g * GB + j + 1)
                            mm = pe.transpose(banks[3 + c][:, j * TOK:(j + 1) * TOK],
                                              rec[0:TOK, slot, j, c * P:(c + 1) * P], ident[0:TOK, 0:TOK])
                        mm.then_inc(S["xn2T_ps"], 1)
                if x2:
                    g, slot, rnd = x2
                    pe.wait_ge(S["qk_sb"], g * 4 + 4)
                    bank_read(pe, (S["rh_sb"], it - 4, it - 3), (S["probs_ready"], it - 3, (it - 3) * GB + GB))
                    for j in range(GB):
                        for c in range(DC):
                            mm = pe.matmul(banks[5][0:TOK, j * TOK:(j + 1) * TOK], qT[:, c, j * TOK:(j + 1) * TOK],
                                           kT[:, c, j * TOK:(j + 1) * TOK], start=(c == 0), stop=(c == DC - 1))
                    mm.then_inc(S["scores_ps"], 1)
                if x0:
                    g, slot, rnd = x0
                    pe.wait_ge(S["xT_sb"], g + 1)
                    for pair in range(2):
                        bank_read(pe, (S["v_ready"], it - 2, (it - 2) * 2 + pair + 1),
                                  (S["ln1"], it - 1, (it - 1) * LN1_N + 2 + 2 * pair))
                        for j in (0, 1):
                            at = (2 * pair + j) * ROWS_X
                            for c in range(DC):
                                mm = pe.matmul(banks[6 + pair][0:TOK, j * D:(j + 1) * D], xT[:, at + c:at + c + TOK],
                                               tokw_sb[:, c, :], start=(c == 0), stop=(c == DC - 1))
                        mm.then_inc(S["tok_ps"], 1)
                if x4:
                    g, slot, rnd = x4
                    pe.wait_ge(S["topk"], g * TOPK_N + 18)
                    bank_read(pe, (S["xn2T_sb"], it - 3, (it - 3) * 2 + 2), (S["pT_sb"], it - 3, it - 2),
                              (S["pos"], it - 5, (it - 5) * POS_N + 1))
                    W = GB * E8
                    pe.matmul(banks[4][0:TOK, 0:W], before[0:TOK, 0:TOK], picked[0:TOK, :], start=True, stop=False,
                              skip_group_check=True)
                    for k in range(1, GB):
                        pe.matmul(banks[4][0:TOK, k * E8:W], ones[0:TOK, 0:TOK], picked[0:TOK, 0:W - k * E8],
                                  start=False, stop=False, skip_group_check=True)
                    for k in range(GB):
                        mm = pe.matmul(banks[4][0:TOK, W:W + E8], ones[0:TOK, 0:TOK], picked[0:TOK, k * E8:(k + 1) * E8],
                                       start=False, stop=(k == GB - 1), skip_group_check=True)
                    mm.then_inc(S["pos_ps"], 1)
                if x1:
                    g, slot, rnd = x1
                    for n, (w, m) in enumerate(((wq_sb, 0), (wq_sb, 1), (wk_sb, 0), (wk_sb, 1))):
                        if n == 0:
                            pe.wait_ge(S["xn1T_sb"], g * 2 + 2)
                            bank_read(pe, (S["xT_sb"], it, it + 1), (S["topk"], it - 4, (it - 4) * TOPK_N + 1),
                                      (S["qk_sb"], it - 2, (it - 2) * 4 + 1))
                        if n == 3:
                            bank_read(pe, (S["xn2T_sb"], it - 3, (it - 3) * 2 + 1), (S["qk_sb"], it - 2, (it - 2) * 4 + 4))
                        for c in range(DC):
                            mm = pe.matmul(banks[n][:, 0:GT], w[:, c, m * P:(m + 1) * P], xn1T[:, c, :],
                                           start=(c == 0), stop=(c == DC - 1))
                        mm.then_inc(S["qk_ps"], 1)
                if x2:
                    g, slot, rnd = x2
                    bank_read(pe, (S["pos"], it - 4, (it - 4) * POS_N + 1), (S["xn2T_sb"], it - 3, (it - 3) * 2 + 2),
                              (S["pT_sb"], it - 3, it - 2))
                    for j in range(GB):
                        pe.wait_ge(S["probs_ready"], g * GB + j + 1)
                        mm = pe.transpose(banks[4][0:TOK, j * TOK:(j + 1) * TOK], probs[0:TOK, j, :],
                                          ident[0:TOK, 0:TOK])
                    mm.then_inc(S["pT_ps"], 1)
                if x3:
                    g, slot, rnd = x3
                    pe.wait_ge(S["xn2T_sb"], g * 2 + 2)
                    bank_read(pe, (S["probs_ready"], it - 2, (it - 2) * GB + GB), (S["rh_sb"], it - 4, it - 3))
                    for c in range(DC):
                        mm = pe.matmul(banks[5][:, 0:GT], rw1_sb[:, c, :], xn2T[:, c, :],
                                       start=(c == 0), stop=(c == DC - 1))
                    mm.then_inc(S["rh_ps"], 1)
                if x2:
                    g, slot, rnd = x2
                    pe.wait_ge(S["pT_sb"], g + 1)
                    pe.wait_ge(S["v_ready"], g * 2 + 2)
                    for pair in range(2):
                        bank_read(pe, (S["qk_sb"], it - 1, (it - 1) * 4 + 2 + pair),
                                  (S["av"], it - 3, (it - 3) * AV_N + 3 + 2 * pair))
                        for j in (0, 1):
                            b = 2 * pair + j
                            mm = pe.matmul(banks[1 + pair][0:TOK, j * D:(j + 1) * D], pT[0:TOK, b * TOK:(b + 1) * TOK],
                                           v_sb[0:TOK, b, :], start=True, stop=True)
                        mm.then_inc(S["av_ps"], 1)
                if x3:
                    g, slot, rnd = x3
                    pe.wait_ge(S["rh_sb"], g + 1)
                    bank_read(pe, (S["qk_sb"], it - 1, (it - 1) * 4 + 1), (S["topk"], it - 4, (it - 4) * TOPK_N + 1))
                    for j in range(GB):
                        mm = pe.matmul(banks[0][0:TOK, j * E8:j * E8 + NE], rhT[:, j * TOK:(j + 1) * TOK], rw2_sb[:],
                                       start=True, stop=True)
                    mm.then_inc(S["logits_ps"], 1)
                if x1:
                    g, slot, rnd = x1
                    for pair in range(2):
                        bank_read(pe, (S["ln1"], it, it * LN1_N + 2 + 2 * pair),
                                  (S["v_ready"], it - 2, (it - 2) * 2 + pair + 1))
                        for j in (0, 1):
                            b = 2 * pair + j
                            for c in range(DC):
                                mm = pe.matmul(banks[6 + pair][0:TOK, j * D:(j + 1) * D],
                                               xn1T[:, c, b * TOK:(b + 1) * TOK], wv_sb[:, c, :],
                                               start=(c == 0), stop=(c == DC - 1))
                        mm.then_inc(S["v_ps"], 1)

            pipeline(pe, step)

            def turn(t, slot, rnd):
                pe.wait_ge(tile_loaded[slot], rnd * 48 + 48)
                for c in range(DC):
                    wait(pe, S["tx_act"], t * 4 - 3 + c)
                    for j in range(TB):
                        mm = pe.transpose(banks[c][:, j * P:(j + 1) * P], xg[:, slot, j, c * P:(c + 1) * P], ident[:])
                    mm.then_inc(S["txT_ps"], 1)

            def layer(slot, n, bank, hi, lo, read, count, done):
                w = w_sb[slot]
                for m in range(DC):
                    wait(pe, read, count + m)
                    for c in range(DC):
                        for p, (wh, act) in enumerate(((0, hi), (0, lo), (1, hi))):
                            mm = pe.matmul(banks[bank + m][:], w[:, n, wh, c, m * P:(m + 1) * P], act[:, c, :],
                                           start=(c == 0 and p == 0), stop=(c == DC - 1 and p == 2))
                    mm.then_inc(done, 1)

            def tile_step(t, slot, rnd):
                inner = not isinstance(t, int)
                if inner or t < NT:
                    pe.wait_ge(S["tx_lo"], t * 2 + 2)
                    pe.wait_ge(S["tx_act"], t * 4 + 4)
                    layer(slot, 0, 2, x_hi, x_lo, S["h1_v"], t * 2 - 1, S["h1_ps"])
                if inner or t + 1 < NT:
                    nxt = (slot + 1) % SLOTS
                    turn(t + 1, nxt, rnd + (slot + 1) // SLOTS)
                if inner or t >= 1:
                    w = w_sb[(slot - 1) % SLOTS]
                    pe.wait_ge(S["h2_split"], t * 4)
                    for b in range(2):
                        wait(pe, S["y_dve"], (t - 1) * 4 - 1 + b)
                        for j in (2 * b, 2 * b + 1):
                            for c in range(DC):
                                for p, (act, wh) in enumerate(((h2_hi, 0), (h2_lo, 0), (h2_hi, 1))):
                                    mm = pe.matmul(banks[6 + b][:, (j % 2) * D:(j % 2 + 1) * D],
                                                   act[:, c, j * P:(j + 1) * P], w[:, 2, wh, c, :],
                                                   start=(c == 0 and p == 0), stop=(c == DC - 1 and p == 2))
                        mm.then_inc(S["y_ps"], 1)
                if inner or t < NT:
                    pe.wait_ge(S["h1_split"], t * 4 + 4)
                    layer(slot, 1, 4, h1_hi, h1_lo, S["h2_v"], t * 2 - 1, S["h2_ps"])

            turn(0, 0, 0)
            tiles(pe, tile_step)

        @block.scalar
        def _(act):
            for n in range(NE * 3):
                act.wait_ge(S[f"raw_w{n % 2}"], 16 * (n // 2 + 1))
                if n >= 2:
                    act.wait_ge(S[f"w_stored{n % 2}"], 16 * (n // 2))
                act.activation(w_sb[n % 2][:, 0, 0, :, :].rearrange("p c n -> p (c n)"),
                               xg[:, n % 2, 0:DC, 0:D], ACT.Identity).then_inc(S["w_high"], 1)
            act.wait_ge(S["const_loaded"], N_CONST)
            act.wait_ge(S["invs"], 2)

            def step(it, group_of):
                x0, x1, x2, x3, x4 = (group_of(s) for s in range(DEPTH))
                if x0:
                    g, slot, rnd = x0
                    act.wait_ge(S["xT_ps"], g + 1)
                    act.activation(xT[:], banks[0][:, 0:GB * ROWS_X], ACT.Identity).then_inc(S["xT_sb"], 1)
                if x1:
                    g, slot, rnd = x1
                    for c in range(DC):
                        act.wait_ge(S["xn1T_ps"], g * 2 + c + 1)
                        act.activation(xn1T[:, c, :], banks[1 + c][:, 0:GT], ACT.Identity).then_inc(S["xn1T_sb"], 1)
                if x3:
                    g, slot, rnd = x3
                    for c in range(DC):
                        act.wait_ge(S["xn2T_ps"], g * 2 + c + 1)
                        act.activation(xn2T[:, c, :], banks[3 + c][:, 0:GT], ACT.Identity).then_inc(S["xn2T_sb"], 1)
                if x2:
                    g, slot, rnd = x2
                    act.wait_ge(S["score_max"], g + 1)
                    for j in range(GB):
                        act.activation(probs[0:TOK, j, :], banks[5][0:TOK, j * TOK:(j + 1) * TOK], ACT.Exp,
                                       bias=negmax[0:TOK, j:j + 1], accum_out=rowsum[0:TOK, j:j + 1]
                                       ).then_inc(S["probs_ready"], 1)
                if x1:
                    g, slot, rnd = x1
                    for n in range(4):
                        act.wait_ge(S["qk_ps"], g * 4 + n + 1)
                        if n < 2:
                            act.activation(qT[:, n, :], banks[n][:, 0:GT], ACT.Identity, bias=bq_col[:, n:n + 1],
                                           scale=invs_col[:, 0:1]).then_inc(S["qk_sb"], 1)
                        else:
                            act.activation(kT[:, n - 2, :], banks[n][:, 0:GT], ACT.Identity,
                                           bias=bk_col[:, n - 2:n - 1]).then_inc(S["qk_sb"], 1)
                if x2:
                    g, slot, rnd = x2
                    act.wait_ge(S["pT_ps"], g + 1)
                    act.activation(pT[0:TOK, :], banks[4][0:TOK, 0:GT], ACT.Identity).then_inc(S["pT_sb"], 1)
                if x3:
                    g, slot, rnd = x3
                    act.wait_ge(S["rh_ps"], g + 1)
                    act.activation(rhT[:], banks[5][:, 0:GT], ACT.Relu, bias=rb1_col[:, 0:1]).then_inc(S["rh_sb"], 1)
                if x0:
                    g, slot, rnd = x0
                    act.wait_ge(S["ln1"], (g + 1) * LN1_N)
                    act.wait_ge(S["rstd2"], g * 2 + 2)
                    wait(act, S["xn1T_ps"], g * 2)
                    for j in range(GB):
                        act.activation(xn1[0:TOK, j, :], h[0:TOK, slot, j, :], ACT.Identity,
                                       bias=nmr[0:TOK, 0, j:j + 1], scale=rstd[0:TOK, 1, j:j + 1]
                                       ).then_inc(S["xn1_ready"], 1)
                if x2:
                    g, slot, rnd = x2
                    act.wait_ge(S["av"], (g + 1) * AV_N)
                    act.wait_ge(S["rstd3"], g * 2 + 2)
                    wait(act, scattered[slot], rnd * (16 * GB * TOPK))
                    for j in range(GB):
                        act.activation(rec[0:TOK, slot, j, 0:D], h[0:TOK, slot, j, :], ACT.Identity,
                                       bias=nmr[0:TOK, 1, j:j + 1], scale=rstd[0:TOK, 2, j:j + 1]
                                       ).then_inc(S["xn2_ready"], 1)
                if x3:
                    g, slot, rnd = x3
                    act.wait_ge(S["topk"], g * TOPK_N + 3)
                    act.activation(pexp[0:TOK, :, :], lshift[0:TOK, :, :], ACT.Exp).then_inc(S["gate_exp"], 1)
                    act.wait_ge(S["topk"], g * TOPK_N + 15)
                    act.activation(gexp[0:TOK, :], gap[0:TOK, :], ACT.Exp).then_inc(S["gate_exp"], 1)

            pipeline(act, step)

            def read_rows(t):
                for c in range(DC):
                    act.wait_ge(S["txT_ps"], t * 2 + c + 1)
                    if c == 0:
                        wait(act, S["tx_lo"], t * 2)
                    act.activation(xv[:, c, :], banks[c][:], ACT.Identity).then_inc(S["tx_act"], 1)
                for c in range(DC):
                    act.wait_ge(S["tx_act"], t * 4 + 1 + c)
                    act.activation(x_hi[:, c, :], xv[:, c, :], ACT.Identity).then_inc(S["tx_act"], 1)

            def tile_step(t, slot, rnd):
                inner = not isinstance(t, int)
                if inner or t < NT:
                    for m in range(DC):
                        act.wait_ge(S["h1_ps"], t * 2 + m + 1)
                        wait(act, S["h1_split"], t * 4 - 2 + 2 * m)
                        act.activation(h1v[:, m, :], banks[2 + m][:], ACT.Relu,
                                       bias=small[:, slot, m:m + 1]).then_inc(S["h1_v"], 1)
                if inner or t + 1 < NT:
                    read_rows(t + 1)
                if inner or t >= 1:
                    for j in range(TB):
                        act.wait_ge(S["y_dve"], (t - 1) * 4 + 3 + j // 2)
                        ys = (slot - 1) % 2
                        act.activation(yo[:, ys, j, :], yo[:, ys, j, :], ACT.Identity,
                                       scale=gcol[:, ys, j:j + 1]).then_inc(S["y_gated"], 1)
                if inner or t < NT:
                    for m in range(DC):
                        act.wait_ge(S["h2_ps"], t * 2 + m + 1)
                        wait(act, S["h2_split"], t * 4 - 2 + 2 * m)
                        act.activation(h2v[:, m, :], banks[4 + m][:], ACT.Relu,
                                       bias=small[:, slot, DC + m:DC + m + 1]).then_inc(S["h2_v"], 1)

            read_rows(0)
            tiles(act, tile_step)

        @block.vector
        def _(v):
            for n in range(NE * 3):
                v.wait_ge(S["w_high"], n + 1)
                v.tensor_tensor(w_sb[n % 2][:, 0, 1, :, :].rearrange("p c n -> p (c n)"), xg[:, n % 2, 0:DC, 0:D],
                                w_sb[n % 2][:, 0, 0, :, :].rearrange("p c n -> p (c n)").bitcast(F32),
                                ALU.subtract).then_inc(S["w_low"], 1)
            v.wait_ge(S["const_loaded"], N_CONST)
            v.wait_ge(S["pool_const"], 15)
            v.reciprocal(invs_col[:], scale_col[:]).then_inc(S["invs"], 1)
            v.wait_ge(S["invs"], 1)
            v.tensor_scalar(bq_col[:], bq_raw[:], invs_col[:, 0:1], None, ALU.mult).then_inc(S["invs"], 1)
            R = slice(0, TOK)

            def statistics(which, src, s, at):
                for j in range(GB):
                    v.wait_ge(s, at - GB + 1 + j)
                    v.bn_stats(stats[R, which, j, :], src(j)).then_inc(s, 1)
                for j in range(GB):
                    wait_apart(v, s, at + 1 + j, S["dve_passed"])
                    v.bn_aggr(mv[R, which, j, :], stats[R, which, j, :]).then_inc(s, 1)

            def step(it, group_of):
                x0, x1, x2, x3, x4 = (group_of(s) for s in range(DEPTH))
                if x2:
                    g, slot, rnd = x2
                    v.wait_ge(S["scores_ps"], g + 1)
                    v.tensor_reduce(negmax[R, :], banks[5][R, 0:GT].rearrange("p (b k) -> p b k", b=GB), AX_X, ALU.max,
                                    negate=True).then_inc(S["score_max"], 1)
                if x0:
                    g, slot, rnd = x0
                    at = g * LN1_N
                    for j in range(GB):
                        v.wait_ge(S["tok_ps"], g * 2 + j // 2 + 1)
                        v.tensor_tensor(y[R, j, :], banks[6 + j // 2][R, (j % 2) * D:(j % 2 + 1) * D], tokb_bc[R, :],
                                        ALU.add).then_inc(S["ln1"], 1)
                    statistics(0, lambda j: y[R, j, :], S["ln1"], at + GB)
                if x4:
                    g, slot, rnd = x4
                    at = g * POS_N
                    v.wait_ge(S["pos_ps"], g + 1)
                    wait(v, S["pos"], at)
                    carry = place[R, (slot - 1) % RING, GB, :]
                    v.tensor_tensor(place[R, slot, :, :],
                                    banks[4][R, 0:(GB + 1) * E8].rearrange("p (b e) -> p b e", e=E8),
                                    carry.unsqueeze(1).to_broadcast([TOK, GB + 1, E8]), ALU.add).then_inc(S["pos"], 1)
                    v.wait_ge(S["pos"], at + 1)
                    v.tensor_tensor(placed[R, :, :, :], onehot[R, :, :, :],
                                    place[R, slot, 0:GB, :].unsqueeze(2).to_broadcast([TOK, GB, TOPK, E8]),
                                    ALU.mult).then_inc(S["pos"], 1)
                    v.wait_ge(S["pos"], at + 2)
                    v.tensor_reduce(rowf[R, :, :], placed[R, :, :, :], AX_X, ALU.add).then_inc(S["pos"], 1)
                    v.wait_ge(S["pos"], at + 3)
                    wait(v, scattered[slot], rnd * (16 * GB * TOPK))
                    v.tensor_copy(row_i[R, slot, :, :], rowf[R, :, :]).then_inc(S["pos"], 1)
                if x0:
                    g, slot, rnd = x0
                    at = g * LN1_N
                    v.wait_ge(S["rstd1"], g * 2 + 2)
                    for j in range(GB):
                        v.scalar_tensor_tensor(out=y[R, j, :], in0=y[R, j, :], scalar=mv[R, 0, j, 0:1],
                                               in1=gamma_bc[R, :], op0=ALU.subtract, op1=ALU.mult).then_inc(S["ln1"], 1)
                    wait(v, h2_stored[slot], rnd * 16)
                    for j in range(GB):
                        v.wait_ge(S["ln1"], at + 3 * GB + 1 + j)
                        v.scalar_tensor_tensor(out=h[R, slot, j, :], in0=y[R, j, :], scalar=rstd[R, 0, j:j + 1],
                                               in1=beta_bc[R, :], op0=ALU.mult, op1=ALU.add).then_inc(S["ln1"], 1)
                    statistics(1, lambda j: h[R, slot, j, :], S["ln1"], at + 5 * GB)
                if x2:
                    g, slot, rnd = x2
                    v.wait_ge(S["probs_ready"], g * GB + GB)
                    v.reciprocal(rinv[R, :], rowsum[R, :]).then_inc(S["av"], 1)
                if x0:
                    g, slot, rnd = x0
                    v.wait_ge(S["rstd2"], g * 2 + 2)
                    v.scalar_tensor_tensor(out=nmr[R, 0, :], in0=mv[R, 1, :, 0], scalar=-1.0, in1=rstd[R, 1, :],
                                           op0=ALU.mult, op1=ALU.mult).then_inc(S["ln1"], 1)
                if x2:
                    g, slot, rnd = x2
                    at = g * AV_N
                    v.wait_ge(S["av"], at + 1)
                    for j in range(GB):
                        v.wait_ge(S["av_ps"], g * 2 + j // 2 + 1)
                        v.scalar_tensor_tensor(out=h[R, slot, j, :],
                                               in0=banks[1 + j // 2][R, (j % 2) * D:(j % 2 + 1) * D],
                                               scalar=rinv[R, j:j + 1], in1=h[R, slot, j, :],
                                               op0=ALU.mult, op1=ALU.add).then_inc(S["av"], 1)
                    statistics(2, lambda j: h[R, slot, j, :], S["av"], at + 1 + GB)
                if x1:
                    g, slot, rnd = x1
                    for pair in range(2):
                        v.wait_ge(S["v_ps"], g * 2 + pair + 1)
                        v.tensor_tensor(v_sb[R, 2 * pair:2 * pair + 2, :],
                                        banks[6 + pair][R, :].rearrange("p (b n) -> p b n", b=2),
                                        bv_bc[R, :].unsqueeze(1).to_broadcast([TOK, 2, D]), ALU.add
                                        ).then_inc(S["v_ready"], 1)
                if x2:
                    g, slot, rnd = x2
                    v.wait_ge(S["rstd3"], g * 2 + 2)
                    v.scalar_tensor_tensor(out=nmr[R, 1, :], in0=mv[R, 2, :, 0], scalar=-1.0, in1=rstd[R, 2, :],
                                           op0=ALU.mult, op1=ALU.mult).then_inc(S["av"], 1)
                if x3:
                    router(*x3)

            def router(g, slot, rnd):
                s = S["topk"]
                at = g * TOPK_N

                def group(col):
                    return col.unsqueeze(2).to_broadcast([TOK, GB, E8])

                v.wait_ge(S["logits_ps"], g + 1)
                v.tensor_tensor(logits[R, :, 0:NE], banks[0][R, 0:GB * E8].rearrange("p (b e) -> p b e", e=E8)[:, :, 0:NE],
                                rb2_bc[R, :].unsqueeze(1).to_broadcast([TOK, GB, NE]), ALU.add).then_inc(s, 1)
                v.wait_ge(s, at + 1)
                v.tensor_reduce(lmax[R, :], logits[R, :, :], AX_X, ALU.max).then_inc(s, 1)
                v.wait_ge(s, at + 2)
                v.tensor_tensor(lshift[R, :, :], logits[R, :, :], group(lmax[R, :]), ALU.subtract).then_inc(s, 1)
                v.wait_ge(S["gate_exp"], g * 2 + 1)
                v.tensor_reduce(psums[R, :], pexp[R, :, :], AX_X, ALU.add).then_inc(s, 1)
                v.wait_ge(s, at + 4)
                v.reciprocal(pinv[R, :], psums[R, :]).then_inc(s, 1)
                v.wait_ge(s, at + 5)
                v.tensor_tensor(pn[R, :, :], pexp[R, :, :], group(pinv[R, :]), ALU.mult).then_inc(s, 1)
                wait_apart(v, s, at + 6, S["dve_passed"])
                for j in range(GB):
                    v.max(mx[R, j, :], pn[R, j, :]).then_inc(s, 1)
                for j in range(GB):
                    wait_apart(v, s, at + 7 + j, S["dve_passed"])
                    v.max_index(mxi[R, j, :], mx[R, j, :], pn[R, j, :]).then_inc(s, 1)
                v.tensor_tensor(gap[R, :], mx[R, :, 1], mx[R, :, 0], ALU.subtract).then_inc(s, 1)
                v.wait_ge(s, at + 14)
                v.tensor_copy(choice[R, :, :], mxi[R, :, 0:TOPK]).then_inc(s, 1)
                v.wait_ge(s, at + 16)
                v.tensor_tensor(onehot[R, :, :, :],
                                iota8[R, :].unsqueeze(1).unsqueeze(1).to_broadcast([TOK, GB, TOPK, E8]),
                                choice[R, :, :].unsqueeze(3).to_broadcast([TOK, GB, TOPK, E8]),
                                ALU.is_equal).then_inc(s, 1)
                v.wait_ge(s, at + 17)
                v.tensor_tensor(picked[R, :].rearrange("p (b e) -> p b e", e=E8), onehot[R, :, 0, :],
                                onehot[R, :, 1, :], ALU.add).then_inc(s, 1)
                v.wait_ge(S["gate_exp"], g * 2 + 2)
                v.tensor_scalar(gden[R, :], gexp[R, :], 1.0, None, ALU.add).then_inc(s, 1)
                v.wait_ge(s, at + 19)
                v.reciprocal(gate2[R, :, 0], gden[R, :]).then_inc(s, 1)
                v.wait_ge(s, at + 20)
                v.tensor_tensor(gate2[R, :, 1], gexp[R, :], gate2[R, :, 0], ALU.mult).then_inc(s, 1)
                v.wait_ge(s, at + 21)
                v.tensor_tensor(gated[R, :, :, :], onehot[R, :, :, :],
                                gate2[R, :, :].unsqueeze(3).to_broadcast([TOK, GB, TOPK, E8]), ALU.mult).then_inc(s, 1)
                v.wait_ge(s, at + 22)
                v.tensor_tensor(rec[R, slot, :, D:D + E8], gated[R, :, 0, :], gated[R, :, 1, :], ALU.add).then_inc(s, 1)
                v.tensor_copy(rec[R, slot, :, D + E8:REC].bitcast(I32), tokid[R, :].unsqueeze(2)).then_inc(s, 1)
                v.tensor_scalar(tokid[R, :], tokid[R, :], float(GT), None, ALU.add).then_inc(s, 1)

            pipeline(v, step)

            s = S["table"]
            n = [0]

            def made(ins):
                ins.then_inc(s, 1)
                n[0] += 1
                v.wait_ge(s, n[0])

            ends = place[0:1, (G - 1) % RING, GB, :]
            v.wait_ge(S["pos"], G * POS_N)
            made(v.tensor_copy(pad_at[:], ends))
            made(v.tensor_tensor(t_nt[:], ends, t_base[:], ALU.subtract))
            made(v.tensor_scalar(t_i[:], t_nt[:], float(TILE - 1), None, ALU.add))
            made(v.tensor_scalar(t_ti[:], t_i[:], TILE.bit_length() - 1, None, ALU.arith_shift_right))
            made(v.tensor_copy(t_nt[:], t_ti[:]))
            made(v.tensor_tensor_scan(t_cum[:], t_nt[:], t_zero[:], 0.0, ALU.add, ALU.add))
            made(v.tensor_scalar(t_delta[:], t_nt[:], -float(TILE), float(REGION), ALU.mult, ALU.add))
            made(v.tensor_tensor(t_ge[:], t_iota[:].unsqueeze(2).to_broadcast([1, NT, E8]),
                                 t_cum[:].unsqueeze(1).to_broadcast([1, NT, E8]), ALU.is_ge))
            made(v.tensor_tensor(t_prod[:], t_ge[:], t_delta[:].unsqueeze(1).to_broadcast([1, NT, E8]), ALU.mult))
            made(v.tensor_reduce(t_row[:], t_prod[:, :, 0:NE], AX_X, ALU.add))
            made(v.scalar_tensor_tensor(out=t_row[:], in0=t_iota[:], scalar=float(TILE), in1=t_row[:],
                                        op0=ALU.mult, op1=ALU.add))
            made(v.tensor_scalar(row_tab[:], t_row[:], float(NE * REGION), None, ALU.min))
            made(v.tensor_reduce(t_exp[:], t_ge[:, :, 0:NE - 1], AX_X, ALU.add))
            v.tensor_copy(exp_tab[:], t_exp[:])
            v.memset(t_load[:, 0:SLOTS], 1.0)
            v.tensor_tensor(t_load[:, SLOTS:NT], t_exp[:, SLOTS:NT], t_exp[:, 0:NT - SLOTS], ALU.not_equal
                            ).then_inc(S["dve_const"], 1)
            v.wait_ge(S["dve_const"], 1)
            v.tensor_copy(load_tab[:], t_load[:]).then_inc(s, 1)

            def split_low(lo, val, hi, ready):
                v.tensor_tensor(lo, val, hi.bitcast(F32), ALU.subtract).then_inc(ready, 1)

            def rows_low(t):
                for c in range(DC):
                    v.wait_ge(S["tx_act"], t * 4 + 3 + c)
                    split_low(x_lo[:, c, :], xv[:, c, :], x_hi[:, c, :], S["tx_lo"])

            def split(t, val, hi, lo, made_by, s):
                for m in range(DC):
                    v.wait_ge(made_by, t * 2 + m + 1)
                    v.tensor_copy(hi[:, m, :], val[:, m, :]).then_inc(s, 1)
                    v.wait_ge(s, t * 4 + 2 * m + 1)
                    split_low(lo[:, m, :], val[:, m, :], hi[:, m, :], s)

            def tile_step(t, slot, rnd):
                inner = not isinstance(t, int)
                if inner or t < NT:
                    split(t, h1v, h1_hi, h1_lo, S["h1_v"], S["h1_split"])
                if inner or t + 1 < NT:
                    rows_low(t + 1)
                if inner or t >= 1:
                    p, ys = (slot - 1) % SLOTS, (slot - 1) % 2
                    at = (t - 1) * 4
                    wait(v, S["y_gated"], (t - 2) * TB)
                    v.tensor_tensor(gsel[:], xg[:, p, :, D:D + E8],
                                    small[:, p, 2 * DC + D:SMALL].unsqueeze(1).to_broadcast([P, TB, E8]),
                                    ALU.mult).then_inc(S["y_dve"], 1)
                    v.wait_ge(S["y_dve"], at + 1)
                    v.tensor_reduce(gcol[:, ys, :], gsel[:], AX_X, ALU.add).then_inc(S["y_dve"], 1)
                    wait(v, S["y_added"], (t - 2) * 16 * TB)
                    for b in range(2):
                        v.wait_ge(S["y_ps"], (t - 1) * 2 + b + 1)
                        v.tensor_tensor(yo[:, ys, 2 * b:2 * b + 2, :],
                                        banks[6 + b][:].rearrange("p (b n) -> p b n", b=2),
                                        small[:, p, 2 * DC:2 * DC + D].unsqueeze(1).to_broadcast([P, 2, D]),
                                        ALU.add).then_inc(S["y_dve"], 1)
                if inner or t < NT:
                    split(t, h2v, h2_hi, h2_lo, S["h2_v"], S["h2_split"])

            rows_low(0)
            tiles(v, tile_step)


def kernel(**inputs):
    import concourse.bacc as bacc
    from concourse.bass_utils import run_bass_kernel_spmd as run

    a = {k: np.asarray(v) for k, v in inputs.items()}

    def columns(v):
        return np.moveaxis(v.reshape(*v.shape[:-1], DC, P), -1, -2)

    onehot = np.broadcast_to(np.eye(NE, E8, dtype=np.float32)[:, None, :], (NE, P, E8))
    small = np.concatenate([columns(a["L0_ffn_expert_b1"]), columns(a["L0_ffn_expert_b2"]),
                            np.broadcast_to(a["L0_ffn_expert_b3"][:, None, :], (NE, P, D)), onehot], axis=2)
    arrays = {
        "x": a["x"].reshape(BATCH, ROWS_X, P),
        "tok_w": a["L0_tok_W"].T, "tok_b": a["L0_tok_b"][None], "tok_gamma": a["L0_tok_gamma"][None],
        "tok_beta": a["L0_tok_beta"][None],
        "wq": a["L0_attn_Wq"].T, "bq": columns(a["L0_attn_bq"]), "wk": a["L0_attn_Wk"].T,
        "bk": columns(a["L0_attn_bk"]), "wv": a["L0_attn_Wv"].T, "bv": a["L0_attn_bv"][None],
        "scale": a["L0_attn_scale"].reshape(1, 1),
        "rw1": a["L0_ffn_router_w1"], "rb1": a["L0_ffn_router_b1"][:, None], "rw2": a["L0_ffn_router_w2"],
        "rb2": a["L0_ffn_router_b2"][None],
        "ew1": a["L0_ffn_expert_w1"], "ew2": a["L0_ffn_expert_w2"], "ew3": a["L0_ffn_expert_w3"],
        "esmall": small,
    }
    nc = bacc.Bacc("TRN2", target_bir_lowering=False, num_devices=1)
    feeds, args = {}, []
    for name, v in arrays.items():
        v = np.ascontiguousarray(v)
        feeds[f"in_{name}"] = v
        args.append(nc.dram_tensor(f"in_{name}", v.shape, mybir.dt.from_np(v.dtype), kind="ExternalInput").ap())
    out = nc.dram_tensor("out", [NTOK, D], F32, kind="ExternalOutput").ap()
    audio_tower(nc, *args, out)
    r = run(nc, [feeds], core_ids=[0])
    return r.results[0]["out"].reshape(BATCH, TOK, D)
```

```python
from contextlib import ExitStack

import numpy as np

import concourse.bass as bass
from concourse import mybir

F32 = mybir.dt.float32
F32R = mybir.dt.float32r
BF16 = mybir.dt.bfloat16
I32 = mybir.dt.int32
U32 = mybir.dt.uint32
ALU = mybir.AluOpType
ACT = mybir.ActivationFunctionType
AX_X = mybir.AxisListType.X

P = 128
BATCH, SEQ, FEAT = 128, 1000, 16
PATCH, STRIDE = 16, 8
TOK = (SEQ - PATCH) // STRIDE + 1
ROWS_X = SEQ * FEAT // P
D = 256
DC = D // P
NE, TOPK = 6, 2
E8 = 8
EPS = 1e-5
GB = 4
G = BATCH // GB
GT = GB * TOK
NTOK = BATCH * TOK
DEPTH = 5
RING = 3

TILE = 512
TB = TILE // P
REGION = NTOK + TILE
NT = (NTOK * TOPK + NE * (TILE - 1)) // TILE
REC = D + E8 + 1
SLOTS = 4
AHEAD = 2
NCHUNK = NE * 3 * DC
assert NCHUNK == G + DEPTH - 1
SMALL = 2 * DC + D + E8

LN1_N, AV_N, TOPK_N, POS_N = 25, 14, 25, 4


def wait(eng, sem, value):
    if isinstance(value, int) and value <= 0:
        return
    eng.wait_ge(sem, value)


def wait_apart(eng, sem, value, passed):
    eng.wait_ge(sem, value)
    eng.sem_inc(passed, 1)


def audio_tower(nc, x, tok_w, tok_b, tok_gamma, tok_beta, wq, bq, wk, bk, wv, bv, scale,
                rw1, rb1, rw2, rb2, eweights, esmall, out):
    with ExitStack() as ctx:
        def sb(name, shape, dt=F32):
            return ctx.enter_context(nc.sbuf_tensor(name, shape, dt))

        def sem(name):
            return ctx.enter_context(nc.semaphore(name))

        banks = [ctx.enter_context(nc.psum_tensor(f"bank{i}", [P, 512], F32)) for i in range(8)]

        rows_dram = nc.dram_tensor("expert_rows", [NE * REGION + TILE, REC], F32, kind="Internal").ap()
        split_dram = nc.dram_tensor("split_weights", [NCHUNK, P, 2 * D], F32, kind="Internal").ap()

        ident = sb("ident", [P, P])
        before = sb("before", [P, P], BF16)
        ones = sb("ones", [P, P], BF16)
        proj = {n: sb(f"{n}_proj", [P, 2, DC, D], F32R) for n in ("tok", "q", "k", "v")}
        bias_row = {n: sb(f"{n}_bias", [P, D], F32R) for n in ("tok", "v")}
        ones_r = sb("ones_r", [P, P], F32R)
        rw1_sb = sb("rw1_sb", [P, DC, P])
        rw2_sb = sb("rw2_sb", [P, NE])
        gamma_bc, beta_bc = sb("gamma_bc", [P, D]), sb("beta_bc", [P, D])
        bq_raw, bk_col, bq_col = (sb(n, [P, DC]) for n in ("bq_raw", "bk_col", "bq_col"))
        rb1_col, scale_col, invs_col = (sb(n, [P, 1]) for n in ("rb1_col", "scale_col", "invs_col"))
        rb2_bc = sb("rb2_bc", [P, NE])
        iota8 = sb("iota8", [P, E8])
        neghalf = sb("neghalf", [P, GB])
        tokid = sb("tokid", [P, GB])
        pad_rows = sb("pad_rows", [P, TB, REC])

        h = sb("h", [P, RING, GB, D])
        rec = sb("rec", [P, RING, GB, REC])
        stats = sb("stats", [P, 3, GB, 6])
        mv = sb("mv", [P, 3, GB, 2])
        vareps = sb("vareps", [P, 3, GB])
        rstd = sb("rstd", [P, 3, GB])
        nmr = sb("nmr", [P, 2, GB])
        negmax, rowsum, rinv = sb("negmax", [P, GB]), sb("rowsum", [P, GB]), sb("rinv", [P, GB])
        logits, lshift, pexp, pn, mx = (sb(n, [P, GB, E8]) for n in ("logits", "lshift", "pexp", "pn", "mx"))
        lmax, psums, pinv = (sb(n, [P, GB]) for n in ("lmax", "psums", "pinv"))
        mxi = sb("mxi", [P, GB, E8], U32)
        gap, gexp, gden = (sb(n, [P, GB]) for n in ("gap", "gexp", "gden"))
        gate2 = sb("gate2", [P, GB, TOPK])
        choice = sb("choice", [P, GB, TOPK])
        onehot = sb("onehot", [P, GB, TOPK, E8])
        gated = sb("gated", [P, GB, TOPK, E8])
        picked = sb("picked", [P, GB * E8], BF16)
        place = sb("place", [P, RING, GB + 1, E8])
        placed = sb("placed", [P, GB, TOPK, E8])
        rowf = sb("rowf", [P, GB, TOPK])
        row_i = sb("row_i", [P, RING, GB, TOPK], I32)
        raw_w = sb("raw_w", [P, RING, D])
        half_w = sb("half_w", [P, RING, 2, D], F32R)

        t_iota = sb("t_iota", [1, NT])
        t_base = sb("t_base", [1, E8])
        t_i = sb("t_i", [1, E8], I32)
        t_ti = sb("t_ti", [1, E8], I32)
        t_nt, t_cum, t_delta = sb("t_nt", [1, E8]), sb("t_cum", [1, E8]), sb("t_delta", [1, E8])
        t_zero = sb("t_zero", [1, E8])
        t_ge, t_prod = sb("t_ge", [1, NT, E8]), sb("t_prod", [1, NT, E8])
        t_row, t_exp, t_load = sb("t_row", [1, NT]), sb("t_exp", [1, NT]), sb("t_load", [1, NT])
        pad_at = sb("pad_at", [1, E8], I32)
        row_tab, exp_tab, load_tab = (sb(n, [1, NT], I32) for n in ("row_tab", "exp_tab", "load_tab"))

        w_sb = [sb(f"w_sb{i}", [P, 3, DC, 2, D], F32R) for i in range(SLOTS)]
        small = sb("small", [P, SLOTS, SMALL])
        xg = sb("xg", [P, SLOTS, TB, REC])

        with ExitStack() as part_a:
            def sba(name, shape, dt=F32):
                return part_a.enter_context(nc.sbuf_tensor(name, shape, dt))

            proj_raw = {n: sba(f"{n}_raw", [P, DC, D]) for n in ("tok", "q", "k", "v")}
            bias_raw = {n: sba(f"{n}_bias_raw", [P, D]) for n in ("tok", "v")}
            x_in = sba("x_in", [P, RING, GB, P])
            xT = sba("xT", [P, GB * ROWS_X])
            xT_hi, xT_lo = sba("xT_hi", [P, GB * ROWS_X], F32R), sba("xT_lo", [P, GB * ROWS_X], F32R)
            y = sba("y", [P, GB, D])
            xn1 = sba("xn1", [P, GB, D])
            xn1T = sba("xn1T", [P, DC, GT])
            xn1T_hi, xn1T_lo = sba("xn1T_hi", [P, DC, GT], F32R), sba("xn1T_lo", [P, DC, GT], F32R)
            qT, kT = sba("qT", [P, DC, GT]), sba("kT", [P, DC, GT])
            v_sb = sba("v_sb", [P, GB, D])
            probs = sba("probs", [P, GB, TOK])
            pT = sba("pT", [P, GB * TOK])
            xn2T = sba("xn2T", [P, DC, GT])
            rhT = sba("rhT", [P, GT])

        xv = sb("xv", [P, DC, TILE])
        x_hi, x_lo = sb("x_hi", [P, DC, TILE], F32R), sb("x_lo", [P, DC, TILE], F32R)
        h1v = sb("h1v", [P, DC, TILE])
        h1_hi, h1_lo = sb("h1_hi", [P, DC, TILE], F32R), sb("h1_lo", [P, DC, TILE], F32R)
        h2v = sb("h2v", [P, DC, TILE])
        h2_hi, h2_lo = sb("h2_hi", [P, DC, TILE], F32R), sb("h2_lo", [P, DC, TILE], F32R)
        yo = sb("yo", [P, 2, TB, D])
        tail = sb("tail", [P, SLOTS, TB, REC - D])
        gsel = sb("gsel", [P, TB, E8])
        gcol = sb("gcol", [P, 2, TB])

        S = {n: sem(n) for n in (
            "tok_loaded", "const_loaded", "pool_const", "dve_const", "invs", "proj_high", "proj_low", "bias_zero",
            "w_high", "w_low", "dummy_cleared", "xT_ps", "xT_sb", "xT_low", "xn1T_low", "tok_ps", "ln1", "rstd1", "rstd2", "rstd3", "xn1_ready", "xn1T_ps", "xn1T_sb",
            "qk_ps", "qk_sb", "v_ps", "v_ready", "scores_ps", "score_max", "probs_ready", "pT_ps", "pT_sb",
            "av_ps", "av", "xn2_ready", "xn2T_ps", "xn2T_sb", "rh_ps", "rh_sb", "logits_ps", "topk", "gate_exp",
            "pos_ps", "pos", "table", "pads_written", "routed",
            "txT_ps", "tx_act", "tx_lo", "h1_ps", "h1_v", "h1_split", "h2_ps", "h2_v", "h2_split",
            "tail_kept", "y_ps", "y_dve", "y_gated", "y_added", "dve_passed", "pool_passed", "sp_passed", "first_loaded")}
        x_loaded = [sem(f"x_loaded{i}") for i in range(RING)]
        h2_stored = [sem(f"h2_stored{i}") for i in range(RING)]
        scattered = [sem(f"scattered{i}") for i in range(RING)]
        raw_loaded = [sem(f"raw_loaded{i}") for i in range(RING)]
        w_stored = [sem(f"w_stored{i}") for i in range(RING)]
        rows_loaded = [sem(f"rows_loaded{i}") for i in range(SLOTS)]
        w_loaded = [sem(f"w_loaded{i}") for i in range(SLOTS)]

        N_TOK = 16 * 3
        N_CONST = 16 * 14

        def uses(slot):
            return (G - slot + RING - 1) // RING

        def pipeline(eng, step, first=0):
            def straight(it):
                def group_of(s):
                    g = it - s
                    return (g, g % RING, g // RING) if 0 <= g < G else None
                step(it, group_of)

            rounds = (G - DEPTH + 1) // RING
            for it in range(DEPTH - 1):
                straight(it)
            with eng.Fori(0, rounds) as k:
                for u in range(RING):
                    c0 = DEPTH - 1 + u

                    def group_of(s, c0=c0):
                        c = c0 - s
                        return k * RING + c, c % RING, k + c // RING
                    step(k * RING + c0, group_of)
            for it in range(DEPTH - 1 + rounds * RING, G + DEPTH - 1):
                straight(it)

        def slot_of(it, group_of):
            return (it % RING, it // RING) if isinstance(it, int) else group_of(0)[1:]

        def bank_read(eng, *uses):
            for s, g, count in uses:
                if not isinstance(g, int) or 0 <= g < G:
                    eng.wait_ge(s, count)
                    return

        def tiles(eng, step):
            head = SLOTS + 1
            rounds = (NT - head) // SLOTS
            for t in range(head):
                step(t, t % SLOTS, t // SLOTS)
            with eng.Fori(0, rounds) as k:
                for u in range(SLOTS):
                    step(k * SLOTS + head + u, (head + u) % SLOTS, k + (head + u) // SLOTS)
            for t in range(head + rounds * SLOTS, NT + 1):
                step(t, t % SLOTS, t // SLOTS)

        block = ctx.enter_context(nc.Block())

        @block.sync
        def _(sp):
            def const(dst, src):
                sp.dma_start(dst, src).then_inc(S["const_loaded"], 16)

            def load_x(g, slot):
                wait(sp, S["xT_ps"], g - RING + 1)
                sp.dma_start(x_in[0:ROWS_X, slot, :, :],
                             x[bass.ds(g * GB, GB), :, :].rearrange("b r n -> r b n")).then_inc(x_loaded[slot], 16)

            def load_chunk(n, slot, rnd):
                wait(sp, S["w_low"], n - RING + 1)
                sp.dma_start(raw_w[:, slot, :], eweights[bass.ds(n, 1), :, :].rearrange("o p n -> (o p) n")
                             ).then_inc(raw_loaded[slot], 16)

            load_x(0, 0)
            sp.dma_start(proj_raw["tok"][:], tok_w.rearrange("(c p) n -> p c n", p=P)).then_inc(S["tok_loaded"], 16)
            for r in (0, 32):
                sp.dma_start(bias_raw["tok"][r:r + 1, :], tok_b).then_inc(S["tok_loaded"], 16)
            const(proj_raw["q"][:], wq.rearrange("(c p) n -> p c n", p=P))
            for r in (0, 32):
                const(bias_raw["v"][r:r + 1, :], bv)
            const(rw1_sb[:], rw1.rearrange("(c p) n -> p c n", p=P))
            const(rw2_sb[:], rw2)
            const(rb2_bc[:], rb2.to_broadcast([P, NE]))
            const(rb1_col[:], rb1)
            load_chunk(0, 0, 0)
            sp.wait_ge(S["pool_const"], 8)
            sp.dma_start(out[NTOK:NTOK + TILE, :].rearrange("(p j) n -> p j n", p=P),
                         pad_rows[:, :, 0:D]).then_inc(S["dummy_cleared"], 16)
            sp.dma_start(rows_dram[NE * REGION:NE * REGION + TILE, :].rearrange("(p j) n -> p (j n)", p=P),
                         pad_rows[:].rearrange("p j n -> p (j n)")).then_inc(S["dummy_cleared"], 16)

            def step(it, group_of):
                loop = not isinstance(it, int)
                slot_it, rnd_it = slot_of(it, group_of)
                if loop or it + 1 < G:
                    load_x(it + 1, (slot_it + 1) % RING)
                if loop or it + 1 < NCHUNK:
                    load_chunk(it + 1, (slot_it + 1) % RING, rnd_it)
                sp.wait_ge(S["w_low"], it + 1)
                sp.wait_ge(S["w_high"], it + 1)
                sp.dma_start(split_dram[bass.ds(it, 1), :, :].rearrange("o p n -> (o p) n"),
                             half_w[:, slot_it, :, :].rearrange("p b n -> p (b n)").bitcast(F32)
                             ).then_inc(w_stored[slot_it], 16)
                if not loop and G - 1 <= it < G - 1 + AHEAD:
                    slot = it - (G - 1)
                    for i in range(RING):
                        sp.wait_ge(w_stored[i], 16 * (3 * DC // RING))
                    sp.dma_start(w_sb[slot][:].rearrange("p a c b n -> p (a c) (b n)").bitcast(F32),
                                 split_dram[0:3 * DC, :, :].rearrange("q p n -> p q n")).then_inc(S["first_loaded"], 16)
                    sp.dma_start(small[:, slot, :], esmall[0, :, :]).then_inc(S["first_loaded"], 16)
                if group_of(2):
                    g, slot, rnd = group_of(2)
                    sp.wait_ge(S["av"], g * AV_N + 1 + GB)
                    sp.dma_start(out[bass.ds(g * GT, GT), :].rearrange("(b p) n -> p b n", p=TOK),
                                 h[0:TOK, slot, :, :]).then_inc(h2_stored[slot], 16)

            pipeline(sp, step)

            sp.wait_ge(S["table"], 1)
            for e in range(NE):
                at = sp.value_load(pad_at[0:1, e:e + 1], min_val=0, max_val=NE * REGION)
                sp.dma_start(rows_dram[bass.ds(at, TILE), :].rearrange("(p j) n -> p (j n)", p=P),
                             pad_rows[:].rearrange("p j n -> p (j n)")).then_inc(S["pads_written"], 16)
            sp.wait_ge(S["table"], 14)
            for i in range(RING):
                sp.wait_ge(w_stored[i], 16 * (NCHUNK // RING))

            def expert_of(t):
                return (sp.value_load(exp_tab[0:1, bass.ds(t, 1)], min_val=0, max_val=NE - 1),
                        sp.value_load(load_tab[0:1, bass.ds(t, 1)], min_val=0, max_val=1))

            def load_weights(slot, expert, fresh):
                sp.dma_start(w_sb[slot][:].rearrange("p a c b n -> p (a c) (b n)").bitcast(F32),
                             split_dram[bass.ds(expert * (3 * DC), 3 * DC), :, :].rearrange("q p n -> p q n"),
                             cond=fresh != 0).then_inc(w_loaded[slot], 16)
                sp.dma_start(small[:, slot, :], esmall[bass.ds(expert, 1), :, :].rearrange("o p n -> (o p) n"),
                             cond=fresh != 0).then_inc(w_loaded[slot], 16)

            def row_of(t):
                return sp.value_load(row_tab[0:1, bass.ds(t, 1)], min_val=0, max_val=NE * REGION)

            def load_rows(slot, row):
                sp.dma_start(xg[:, slot, :, :].rearrange("p j n -> p (j n)"),
                             rows_dram[bass.ds(row, TILE), :].rearrange("(p j) n -> p (j n)", p=P)
                             ).then_inc(rows_loaded[slot], 16)

            sp.wait_ge(S["first_loaded"], 32 * AHEAD)
            load_weights(0, *expert_of(0))
            first_rows = [row_of(t) for t in range(SLOTS)]
            first_experts = [expert_of(t) for t in range(1, SLOTS)]
            for i in range(RING):
                sp.wait_ge(h2_stored[i], 16 * uses(i))
                sp.wait_ge(scattered[i], 16 * GB * TOPK * uses(i))
            sp.wait_ge(S["dummy_cleared"], 32)
            sp.wait_ge(S["pads_written"], 16 * NE)
            sp.sem_inc(S["routed"], 1)
            load_rows(0, first_rows[0])
            for t in range(1, SLOTS):
                load_rows(t, first_rows[t])
                load_weights(t, *first_experts[t - 1])

            def load_tile(t, slot, rnd):
                if isinstance(t, int) and (t < SLOTS or t >= NT):
                    return
                wait_apart(sp, S["txT_ps"], (t - SLOTS + 1) * 2, S["sp_passed"])
                wait_apart(sp, S["tail_kept"], (t - SLOTS + 1) * 2, S["sp_passed"])
                load_rows(slot, row_of(t))
                wait_apart(sp, S["y_dve"], (t - SLOTS + 1) * 4, S["sp_passed"])
                load_weights(slot, *expert_of(t))

            tiles(sp, load_tile)
            sp.wait_ge(S["y_added"], NT * 16 * TB)

        @block.gpsimd
        def _(pool):
            done = S["pool_const"]
            pool.memset(ident[:], 0.0).then_inc(done, 1)
            pool.memset(before[:], 0.0).then_inc(done, 1)
            pool.memset(ones[:], 1.0).then_inc(done, 1)
            pool.memset(pad_rows[:], 0.0).then_inc(done, 1)
            pool.wait_ge(done, 4)
            pool.affine_select(out=ident[:], in_=ident[:], compare_op=ALU.not_equal, fill=1.0, base=0,
                               pattern=[[-1, P]], channel_multiplier=1).then_inc(done, 1)
            pool.affine_select(out=before[:], in_=before[:], compare_op=ALU.is_ge, fill=1.0, base=0,
                               pattern=[[-1, P]], channel_multiplier=1).then_inc(done, 1)
            pool.iota(pad_rows[:, :, D + E8:REC].bitcast(I32).rearrange("p j o -> p (j o)"), [[1, TB]], base=NTOK,
                      channel_multiplier=TB).then_inc(done, 1)
            pool.memset(neghalf[:], -0.5).then_inc(done, 1)
            pool.iota(iota8[:], [[1, E8]], base=0, channel_multiplier=0,
                      allow_small_or_imprecise_dtypes=True).then_inc(done, 1)
            pool.iota(tokid[:], [[TOK, GB]], base=0, channel_multiplier=1,
                      allow_small_or_imprecise_dtypes=True).then_inc(done, 1)
            pool.iota(place[:, RING - 1, GB, :], [[REGION, E8]], base=0, channel_multiplier=0,
                      allow_small_or_imprecise_dtypes=True).then_inc(done, 1)
            pool.iota(t_iota[:], [[1, NT]], base=0, channel_multiplier=0,
                      allow_small_or_imprecise_dtypes=True).then_inc(done, 1)
            pool.iota(t_base[:], [[REGION, E8]], base=0, channel_multiplier=0,
                      allow_small_or_imprecise_dtypes=True).then_inc(done, 1)
            pool.memset(t_zero[:], 0.0).then_inc(done, 1)
            pool.memset(logits[:], -1e30).then_inc(done, 1)
            pool.memset(ones_r[:].bitcast(F32), 1.0).then_inc(done, 1)
            for n in ("tok", "v"):
                pool.memset(bias_row[n][:].bitcast(F32), 0.0).then_inc(done, 1)

            def inverse_std(which, ready, g):
                pool.tensor_scalar(vareps[0:TOK, which, :], mv[0:TOK, which, :, 1], EPS, None,
                                   ALU.add).then_inc(ready, 1)
                pool.wait_ge(ready, g * 2 + 1)
                pool.tensor_tensor(rstd[0:TOK, which, :], vareps[0:TOK, which, :], neghalf[0:TOK, :],
                                   ALU.pow).then_inc(ready, 1)

            def step(it, group_of):
                if group_of(0):
                    g, slot, rnd = group_of(0)
                    wait_apart(pool, S["ln1"], g * LN1_N + 2 * GB, S["pool_passed"])
                    inverse_std(0, S["rstd1"], g)
                    wait(pool, S["xn1_ready"], g * GB)
                    wait_apart(pool, S["ln1"], g * LN1_N + 6 * GB, S["pool_passed"])
                    inverse_std(1, S["rstd2"], g)
                if group_of(2):
                    g, slot, rnd = group_of(2)
                    wait(pool, S["xn2_ready"], g * GB)
                    wait_apart(pool, S["av"], g * AV_N + 1 + 3 * GB, S["pool_passed"])
                    inverse_std(2, S["rstd3"], g)
                if group_of(4):
                    g, slot, rnd = group_of(4)
                    pool.wait_ge(S["pos"], (g + 1) * POS_N)
                    pool.wait_ge(S["topk"], (g + 1) * TOPK_N)
                    wait_apart(pool, S["xn2_ready"], (g + 1) * GB, S["pool_passed"])
                    for j in range(GB):
                        for k in range(TOPK):
                            pool.indirect_dma_start(
                                rows_dram, bass.IndirectOffsetOnAxis(ap=row_i[0:TOK, slot, j, k:k + 1], axis=0),
                                rec[0:TOK, slot, j, :], None).then_inc(scattered[slot], 16)

            pipeline(pool, step)

            pool.wait_ge(S["routed"], 1)

            def add_tile(t, slot, rnd):
                if isinstance(t, int) and t == 0:
                    return
                s = (slot - 1) % SLOTS
                ys = (slot - 1) % 2
                wait(pool, S["y_added"], (t - 1) * 16 * TB)
                wait_apart(pool, S["y_gated"], t * TB, S["pool_passed"])
                for j in range(TB):
                    pool.indirect_dma_start(
                        out, bass.IndirectOffsetOnAxis(ap=tail[:, s, j, E8:].bitcast(I32), axis=0),
                        yo[:, ys, j, :], None, compute_op=ALU.add).then_inc(S["y_added"], 16)

            tiles(pool, add_tile)

        @block.tensor
        def _(pe):
            pe.wait_ge(S["pool_const"], 18)

            def product(bank, lhs, rhs, first, last):
                for n, (a, b) in enumerate(((0, 0), (0, 1), (1, 0))):
                    mm = pe.matmul(bank, lhs[a], rhs[b], start=(first and n == 0), stop=(last and n == 2))
                return mm

            def step(it, group_of):
                x0, x1, x2, x3, x4 = (group_of(s) for s in range(DEPTH))
                if x0:
                    g, slot, rnd = x0
                    pe.wait_ge(x_loaded[slot], rnd * 16 + 16)
                    bank_read(pe, (S["qk_sb"], it - 2, (it - 2) * 4 + 1), (S["xT_sb"], it - 1, it * 2 - 1))
                    for j in range(GB):
                        mm = pe.transpose(banks[0][:, j * ROWS_X:(j + 1) * ROWS_X],
                                          x_in[0:ROWS_X, slot, j, :], ident[0:ROWS_X, 0:ROWS_X])
                    mm.then_inc(S["xT_ps"], 1)
                if x1:
                    g, slot, rnd = x1
                    for c in range(DC):
                        bank_read(pe, (S["av"], it - 3, (it - 3) * AV_N + 3 + 2 * c),
                                  (S["qk_sb"], it - 2, (it - 2) * 4 + 2 + c))
                        for j in range(GB):
                            pe.wait_ge(S["xn1_ready"], g * GB + j + 1)
                            mm = pe.transpose(banks[1 + c][:, j * TOK:(j + 1) * TOK],
                                              xn1[0:TOK, j, c * P:(c + 1) * P], ident[0:TOK, 0:TOK])
                        mm.then_inc(S["xn1T_ps"], 1)
                if x2:
                    g, slot, rnd = x2
                    pe.wait_ge(S["qk_sb"], g * 4 + 4)
                    bank_read(pe, (S["topk"], it - 4, (it - 4) * TOPK_N + 1), (S["probs_ready"], it - 3, (it - 3) * GB + GB))
                    for j in range(GB):
                        for c in range(DC):
                            mm = pe.matmul(banks[5][0:TOK, j * TOK:(j + 1) * TOK], qT[:, c, j * TOK:(j + 1) * TOK],
                                           kT[:, c, j * TOK:(j + 1) * TOK], start=(c == 0), stop=(c == DC - 1))
                    mm.then_inc(S["scores_ps"], 1)
                if x0:
                    g, slot, rnd = x0
                    pe.wait_ge(S["xT_sb"], g * 2 + 2)
                    pe.wait_ge(S["xT_low"], g + 1)
                    if isinstance(it, int) and it == 0:
                        pe.wait_ge(S["proj_low"], 2)
                    for pair in range(2):
                        bank_read(pe, (S["v_ready"], it - 2, (it - 2) * 2 + pair + 1),
                                  (S["ln1"], it - 1, (it - 1) * LN1_N + 2 * GB + 2 + 2 * pair))
                        for j in (0, 1):
                            at = (2 * pair + j) * ROWS_X
                            into = banks[6 + pair][0:TOK, j * D:(j + 1) * D]
                            for c in range(DC):
                                product(into, [t[:, at + c:at + c + TOK] for t in (xT_hi, xT_lo)],
                                        [proj["tok"][:, b, c, :] for b in range(2)], c == 0, False)
                            mm = pe.matmul(into, ones_r[:, 0:TOK], bias_row["tok"][:], start=False, stop=True)
                        mm.then_inc(S["tok_ps"], 1)
                if x3:
                    g, slot, rnd = x3
                    for c in range(DC):
                        if c == 0:
                            bank_read(pe, (S["qk_sb"], it - 2, (it - 2) * 4 + 4), (S["xn2T_sb"], it - 4, (it - 4) * 2 + 1))
                        else:
                            bank_read(pe, (S["pT_sb"], it - 3, it - 2), (S["pos"], it - 5, (it - 5) * POS_N + 1),
                                      (S["xn2T_sb"], it - 4, (it - 4) * 2 + 2))
                        for j in range(GB):
                            pe.wait_ge(S["xn2_ready"], g * GB + j + 1)
                            mm = pe.transpose(banks[3 + c][:, j * TOK:(j + 1) * TOK],
                                              rec[0:TOK, slot, j, c * P:(c + 1) * P], ident[0:TOK, 0:TOK])
                        mm.then_inc(S["xn2T_ps"], 1)
                def projections(g, outputs):
                    for n in outputs:
                        w, m = "qqkk"[n], n % 2
                        if n == 0:
                            pe.wait_ge(S["xn1T_sb"], g * 4 + 4)
                            pe.wait_ge(S["xn1T_low"], g * 2 + 2)
                            bank_read(pe, (S["xT_sb"], it, it * 2 + 1), (S["qk_sb"], it - 2, (it - 2) * 4 + 1))
                        if n == 3:
                            bank_read(pe, (S["xn2T_sb"], it - 3, (it - 3) * 2 + 1), (S["qk_sb"], it - 2, (it - 2) * 4 + 4))
                        for c in range(DC):
                            mm = product(banks[n][:, 0:GT], [proj[w][:, b, c, m * P:(m + 1) * P] for b in range(2)],
                                         [xn1T_hi[:, c, :], xn1T_lo[:, c, :]], c == 0, c == DC - 1)
                        mm.then_inc(S["qk_ps"], 1)
                if isinstance(it, int) and it == 1:
                    pe.wait_ge(S["const_loaded"], N_CONST)
                    pe.wait_ge(S["proj_low"], 6)
                if x1:
                    projections(x1[0], (0, 1))
                if x4:
                    g, slot, rnd = x4
                    pe.wait_ge(S["topk"], g * TOPK_N + 18)
                    bank_read(pe, (S["xn2T_sb"], it - 3, (it - 3) * 2 + 2), (S["pT_sb"], it - 3, it - 2),
                              (S["pos"], it - 5, (it - 5) * POS_N + 1))
                    W = GB * E8
                    pe.matmul(banks[4][0:TOK, 0:W], before[0:TOK, 0:TOK], picked[0:TOK, :], start=True, stop=False,
                              skip_group_check=True)
                    for k in range(1, GB):
                        pe.matmul(banks[4][0:TOK, k * E8:W], ones[0:TOK, 0:TOK], picked[0:TOK, 0:W - k * E8],
                                  start=False, stop=False, skip_group_check=True)
                    for k in range(GB):
                        mm = pe.matmul(banks[4][0:TOK, W:W + E8], ones[0:TOK, 0:TOK], picked[0:TOK, k * E8:(k + 1) * E8],
                                       start=False, stop=(k == GB - 1), skip_group_check=True)
                    mm.then_inc(S["pos_ps"], 1)
                if x1:
                    projections(x1[0], (2, 3))
                if x2:
                    g, slot, rnd = x2
                    bank_read(pe, (S["pos"], it - 4, (it - 4) * POS_N + 1), (S["xn2T_sb"], it - 3, (it - 3) * 2 + 2),
                              (S["pT_sb"], it - 3, it - 2))
                    for j in range(GB):
                        pe.wait_ge(S["probs_ready"], g * GB + j + 1)
                        mm = pe.transpose(banks[4][0:TOK, j * TOK:(j + 1) * TOK], probs[0:TOK, j, :],
                                          ident[0:TOK, 0:TOK])
                    mm.then_inc(S["pT_ps"], 1)
                if x3:
                    g, slot, rnd = x3
                    pe.wait_ge(S["xn2T_sb"], g * 2 + 2)
                    bank_read(pe, (S["probs_ready"], it - 2, (it - 2) * GB + GB), (S["topk"], it - 4, (it - 4) * TOPK_N + 1))
                    for c in range(DC):
                        mm = pe.matmul(banks[5][:, 0:GT], rw1_sb[:, c, :], xn2T[:, c, :],
                                       start=(c == 0), stop=(c == DC - 1))
                    mm.then_inc(S["rh_ps"], 1)
                if x2:
                    g, slot, rnd = x2
                    pe.wait_ge(S["pT_sb"], g + 1)
                    pe.wait_ge(S["v_ready"], g * 2 + 2)
                    for pair in range(2):
                        bank_read(pe, (S["qk_sb"], it - 1, (it - 1) * 4 + 2 + pair),
                                  (S["av"], it - 3, (it - 3) * AV_N + 3 + 2 * pair))
                        for j in (0, 1):
                            b = 2 * pair + j
                            mm = pe.matmul(banks[1 + pair][0:TOK, j * D:(j + 1) * D], pT[0:TOK, b * TOK:(b + 1) * TOK],
                                           v_sb[0:TOK, b, :], start=True, stop=True)
                        mm.then_inc(S["av_ps"], 1)
                if x3:
                    g, slot, rnd = x3
                    pe.wait_ge(S["rh_sb"], g + 1)
                    for j in range(GB):
                        mm = pe.matmul(banks[5][0:TOK, j * E8:j * E8 + NE], rhT[:, j * TOK:(j + 1) * TOK], rw2_sb[:],
                                       start=True, stop=True)
                    mm.then_inc(S["logits_ps"], 1)
                if x1:
                    g, slot, rnd = x1
                    for pair in range(2):
                        bank_read(pe, (S["ln1"], it, it * LN1_N + 2 * GB + 2 + 2 * pair),
                                  (S["v_ready"], it - 2, (it - 2) * 2 + pair + 1))
                        for j in (0, 1):
                            b = 2 * pair + j
                            into = banks[6 + pair][0:TOK, j * D:(j + 1) * D]
                            for c in range(DC):
                                product(into, [t[:, c, b * TOK:(b + 1) * TOK] for t in (xn1T_hi, xn1T_lo)],
                                        [proj["v"][:, b2, c, :] for b2 in range(2)], c == 0, False)
                            mm = pe.matmul(into, ones_r[:, 0:TOK], bias_row["v"][:], start=False, stop=True)
                        mm.then_inc(S["v_ps"], 1)

            pipeline(pe, step)

            def turn(t, slot, rnd):
                pe.wait_ge(rows_loaded[slot], rnd * 16 + 16)
                for c in range(DC):
                    wait(pe, S["tx_act"], t * 4 - 3 + c)
                    for j in range(TB):
                        mm = pe.transpose(banks[c][:, j * P:(j + 1) * P], xg[:, slot, j, c * P:(c + 1) * P], ident[:])
                    mm.then_inc(S["txT_ps"], 1)

            def layer(slot, n, bank, hi, lo, read, count, done):
                w = w_sb[slot]
                for m in range(DC):
                    wait(pe, read, count + m)
                    for c in range(DC):
                        for p, (wh, act) in enumerate(((0, hi), (0, lo), (1, hi))):
                            mm = pe.matmul(banks[bank + m][:], w[:, n, c, wh, m * P:(m + 1) * P], act[:, c, :],
                                           start=(c == 0 and p == 0), stop=(c == DC - 1 and p == 2))
                    mm.then_inc(done, 1)

            def tile_step(t, slot, rnd):
                inner = not isinstance(t, int)
                if inner or t < NT:
                    pe.wait_ge(w_loaded[slot], rnd * 32 + 32)
                    pe.wait_ge(S["tx_lo"], t * 2 + 2)
                    pe.wait_ge(S["tx_act"], t * 4 + 4)
                    layer(slot, 0, 2, x_hi, x_lo, S["h1_v"], t * 2 - 1, S["h1_ps"])
                if inner or t + 1 < NT:
                    nxt = (slot + 1) % SLOTS
                    turn(t + 1, nxt, rnd + (slot + 1) // SLOTS)
                if inner or t >= 1:
                    w = w_sb[(slot - 1) % SLOTS]
                    pe.wait_ge(S["h2_split"], t * 4)
                    for b in range(2):
                        wait(pe, S["y_dve"], (t - 1) * 4 - 1 + b)
                        for j in (2 * b, 2 * b + 1):
                            for c in range(DC):
                                for p, (act, wh) in enumerate(((h2_hi, 0), (h2_lo, 0), (h2_hi, 1))):
                                    mm = pe.matmul(banks[6 + b][:, (j % 2) * D:(j % 2 + 1) * D],
                                                   act[:, c, j * P:(j + 1) * P], w[:, 2, c, wh, :],
                                                   start=(c == 0 and p == 0), stop=(c == DC - 1 and p == 2))
                        mm.then_inc(S["y_ps"], 1)
                if inner or t < NT:
                    pe.wait_ge(S["h1_split"], t * 4 + 4)
                    layer(slot, 1, 4, h1_hi, h1_lo, S["h2_v"], t * 2 - 1, S["h2_ps"])

            turn(0, 0, 0)
            tiles(pe, tile_step)

        @block.scalar
        def _(act):
            def const(dst, src):
                act.dma_start(dst, src).then_inc(S["const_loaded"], 16)

            for n, src in (("k", wk), ("v", wv)):
                const(proj_raw[n][:], src.rearrange("(c p) n -> p c n", p=P))
            for dst, src in ((gamma_bc, tok_gamma), (beta_bc, tok_beta)):
                const(dst[:], src.to_broadcast([P, D]))
            const(bq_raw[:], bq)
            const(bk_col[:], bk)
            const(scale_col[:], scale.to_broadcast([P, 1]))
            def high_halves(n):
                act.activation(proj[n][:, 0, :, :], proj_raw[n][:], ACT.Identity).then_inc(S["proj_high"], 1)

            def high_bias(n):
                for r in (0, 32):
                    act.activation(bias_row[n][r:r + 1, :], bias_raw[n][r:r + 1, :], ACT.Identity
                                   ).then_inc(S["proj_high"], 1)

            act.wait_ge(S["tok_loaded"], N_TOK)
            act.wait_ge(S["pool_const"], 18)
            high_halves("tok")
            high_bias("tok")

            def step(it, group_of):
                x0, x1, x2, x3, x4 = (group_of(s) for s in range(DEPTH))
                if x0:
                    g, slot, rnd = x0
                    act.wait_ge(S["xT_ps"], g + 1)
                    wait(act, S["xT_low"], g)
                    act.activation(xT[:], banks[0][:, 0:GB * ROWS_X], ACT.Identity).then_inc(S["xT_sb"], 1)
                    act.wait_ge(S["xT_sb"], g * 2 + 1)
                    act.activation(xT_hi[:], xT[:], ACT.Identity).then_inc(S["xT_sb"], 1)
                if isinstance(it, int) and it == 0:
                    act.wait_ge(S["const_loaded"], N_CONST)
                    for n in ("q", "k", "v"):
                        high_halves(n)
                    high_bias("v")
                    act.wait_ge(S["invs"], 2)
                if x4:
                    g, slot, rnd = x4
                    act.wait_ge(S["topk"], g * TOPK_N + 3)
                    act.activation(pexp[0:TOK, :, :], lshift[0:TOK, :, :], ACT.Exp).then_inc(S["gate_exp"], 1)
                if x1:
                    g, slot, rnd = x1
                    for c in range(DC):
                        act.wait_ge(S["xn1T_ps"], g * 2 + c + 1)
                        wait(act, S["xn1T_low"], g * 2 - 1 + c)
                        act.activation(xn1T[:, c, :], banks[1 + c][:, 0:GT], ACT.Identity).then_inc(S["xn1T_sb"], 1)
                    for c in range(DC):
                        act.wait_ge(S["xn1T_sb"], g * 4 + 1 + c)
                        act.activation(xn1T_hi[:, c, :], xn1T[:, c, :], ACT.Identity).then_inc(S["xn1T_sb"], 1)
                if x3:
                    g, slot, rnd = x3
                    act.wait_ge(S["av"], (g + 1) * AV_N)
                    act.wait_ge(S["rstd3"], g * 2 + 2)
                    wait(act, scattered[slot], rnd * (16 * GB * TOPK))
                    for j in range(GB):
                        act.activation(rec[0:TOK, slot, j, 0:D], h[0:TOK, slot, j, :], ACT.Identity,
                                       bias=nmr[0:TOK, 1, j:j + 1], scale=rstd[0:TOK, 2, j:j + 1]
                                       ).then_inc(S["xn2_ready"], 1)
                if x2:
                    g, slot, rnd = x2
                    act.wait_ge(S["score_max"], g + 1)
                    for j in range(GB):
                        act.activation(probs[0:TOK, j, :], banks[5][0:TOK, j * TOK:(j + 1) * TOK], ACT.Exp,
                                       bias=negmax[0:TOK, j:j + 1], accum_out=rowsum[0:TOK, j:j + 1]
                                       ).then_inc(S["probs_ready"], 1)
                if x3:
                    g, slot, rnd = x3
                    for c in range(DC):
                        act.wait_ge(S["xn2T_ps"], g * 2 + c + 1)
                        act.activation(xn2T[:, c, :], banks[3 + c][:, 0:GT], ACT.Identity).then_inc(S["xn2T_sb"], 1)
                if x4:
                    g, slot, rnd = x4
                    act.wait_ge(S["topk"], g * TOPK_N + 15)
                    act.activation(gexp[0:TOK, :], gap[0:TOK, :], ACT.Exp).then_inc(S["gate_exp"], 1)
                if x1:
                    g, slot, rnd = x1
                    for n in range(4):
                        act.wait_ge(S["qk_ps"], g * 4 + n + 1)
                        if n < 2:
                            act.activation(qT[:, n, :], banks[n][:, 0:GT], ACT.Identity, bias=bq_col[:, n:n + 1],
                                           scale=invs_col[:, 0:1]).then_inc(S["qk_sb"], 1)
                        else:
                            act.activation(kT[:, n - 2, :], banks[n][:, 0:GT], ACT.Identity,
                                           bias=bk_col[:, n - 2:n - 1]).then_inc(S["qk_sb"], 1)
                if x2:
                    g, slot, rnd = x2
                    act.wait_ge(S["pT_ps"], g + 1)
                    act.activation(pT[0:TOK, :], banks[4][0:TOK, 0:GT], ACT.Identity).then_inc(S["pT_sb"], 1)
                if x3:
                    g, slot, rnd = x3
                    act.wait_ge(S["rh_ps"], g + 1)
                    act.activation(rhT[:], banks[5][:, 0:GT], ACT.Relu, bias=rb1_col[:, 0:1]).then_inc(S["rh_sb"], 1)
                slot_it, rnd_it = slot_of(it, group_of)
                act.wait_ge(raw_loaded[slot_it], rnd_it * 16 + 16)
                wait(act, w_stored[slot_it], rnd_it * 16)
                act.activation(half_w[:, slot_it, 0, :], raw_w[:, slot_it, :], ACT.Identity).then_inc(S["w_high"], 1)
                if x0:
                    g, slot, rnd = x0
                    act.wait_ge(S["ln1"], (g + 1) * LN1_N)
                    act.wait_ge(S["rstd2"], g * 2 + 2)
                    wait(act, S["xn1T_ps"], g * 2)
                    for j in range(GB):
                        act.activation(xn1[0:TOK, j, :], h[0:TOK, slot, j, :], ACT.Identity,
                                       bias=nmr[0:TOK, 0, j:j + 1], scale=rstd[0:TOK, 1, j:j + 1]
                                       ).then_inc(S["xn1_ready"], 1)
                if x1:
                    g, slot, rnd = x1
                    for pair in range(2):
                        act.wait_ge(S["v_ps"], g * 2 + pair + 1)
                        act.activation(v_sb[0:TOK, 2 * pair:2 * pair + 2, :],
                                       banks[6 + pair][0:TOK, :].rearrange("p (b n) -> p b n", b=2),
                                       ACT.Identity).then_inc(S["v_ready"], 1)

            pipeline(act, step)

            def read_rows(t):
                for c in range(DC):
                    act.wait_ge(S["txT_ps"], t * 2 + c + 1)
                    if c == 0:
                        wait(act, S["tx_lo"], t * 2)
                    act.activation(xv[:, c, :], banks[c][:], ACT.Identity).then_inc(S["tx_act"], 1)
                for c in range(DC):
                    act.wait_ge(S["tx_act"], t * 4 + 1 + c)
                    act.activation(x_hi[:, c, :], xv[:, c, :], ACT.Identity).then_inc(S["tx_act"], 1)

            def tile_step(t, slot, rnd):
                inner = not isinstance(t, int)
                if inner or t < NT:
                    for m in range(DC):
                        if m == 0:
                            act.wait_ge(w_loaded[slot], rnd * 32 + 32)
                        act.wait_ge(S["h1_ps"], t * 2 + m + 1)
                        wait(act, S["h1_split"], t * 4 - 2 + 2 * m)
                        act.activation(h1v[:, m, :], banks[2 + m][:], ACT.Relu,
                                       bias=small[:, slot, m:m + 1]).then_inc(S["h1_v"], 1)
                if inner or t + 1 < NT:
                    read_rows(t + 1)
                if inner or t < NT:
                    for m in range(DC):
                        act.wait_ge(S["h2_ps"], t * 2 + m + 1)
                        wait(act, S["h2_split"], t * 4 - 2 + 2 * m)
                        act.activation(h2v[:, m, :], banks[4 + m][:], ACT.Relu,
                                       bias=small[:, slot, DC + m:DC + m + 1]).then_inc(S["h2_v"], 1)
                if inner or t >= 1:
                    for j in range(TB):
                        act.wait_ge(S["y_dve"], (t - 1) * 4 + 3 + j // 2)
                        ys = (slot - 1) % 2
                        act.activation(yo[:, ys, j, :], yo[:, ys, j, :], ACT.Identity,
                                       scale=gcol[:, ys, j:j + 1]).then_inc(S["y_gated"], 1)

            read_rows(0)
            tiles(act, tile_step)

        @block.vector
        def _(v):
            def low_halves(n, high):
                v.wait_ge(S["proj_high"], high)
                v.tensor_tensor(proj[n][:, 1, :, :], proj_raw[n][:], proj[n][:, 0, :, :].bitcast(F32),
                                ALU.subtract).then_inc(S["proj_low"], 1)

            def low_bias(n, high):
                v.wait_ge(S["proj_high"], high)
                v.tensor_tensor(bias_row[n][32:33, :], bias_raw[n][32:33, :], bias_row[n][32:33, :].bitcast(F32),
                                ALU.subtract).then_inc(S["proj_low"], 1)

            v.wait_ge(S["tok_loaded"], N_TOK)
            v.wait_ge(S["pool_const"], 18)
            low_halves("tok", 1)
            low_bias("tok", 3)
            R = slice(0, TOK)

            def embedded(j):
                return banks[6 + j // 2][R, (j % 2) * D:(j % 2 + 1) * D]

            def statistics(which, src, s, at, g):
                for j in range(GB):
                    if which == 0:
                        v.wait_ge(S["tok_ps"], g * 2 + j // 2 + 1)
                    else:
                        v.wait_ge(s, at - GB + 1 + j)
                    v.bn_stats(stats[R, which, j, :], src(j)).then_inc(s, 1)
                for j in range(GB):
                    wait_apart(v, s, at + 1 + j, S["dve_passed"])
                    v.bn_aggr(mv[R, which, j, :], stats[R, which, j, :]).then_inc(s, 1)

            def step(it, group_of):
                x0, x1, x2, x3, x4 = (group_of(s) for s in range(DEPTH))
                if x0:
                    g, slot, rnd = x0
                    v.wait_ge(S["xT_sb"], g * 2 + 2)
                    v.tensor_tensor(xT_lo[:], xT[:], xT_hi[:].bitcast(F32), ALU.subtract).then_inc(S["xT_low"], 1)
                if isinstance(it, int) and it == 0:
                    v.wait_ge(S["const_loaded"], N_CONST)
                    v.reciprocal(invs_col[:], scale_col[:]).then_inc(S["invs"], 1)
                    v.wait_ge(S["invs"], 1)
                    v.tensor_scalar(bq_col[:], bq_raw[:], invs_col[:, 0:1], None, ALU.mult).then_inc(S["invs"], 1)
                    for n, name in enumerate(("q", "k", "v")):
                        low_halves(name, 4 + n)
                    low_bias("v", 8)
                if x3:
                    g, slot, rnd = x3
                    v.wait_ge(S["rstd3"], g * 2 + 2)
                    v.scalar_tensor_tensor(out=nmr[R, 1, :], in0=mv[R, 2, :, 0], scalar=-1.0, in1=rstd[R, 2, :],
                                           op0=ALU.mult, op1=ALU.mult).then_inc(S["av"], 1)
                if x2:
                    g, slot, rnd = x2
                    v.wait_ge(S["scores_ps"], g + 1)
                    v.tensor_reduce(negmax[R, :], banks[5][R, 0:GT].rearrange("p (b k) -> p b k", b=GB), AX_X, ALU.max,
                                    negate=True).then_inc(S["score_max"], 1)
                if x1:
                    g, slot, rnd = x1
                    for c in range(DC):
                        v.wait_ge(S["xn1T_sb"], g * 4 + 3 + c)
                        v.tensor_tensor(xn1T_lo[:, c, :], xn1T[:, c, :], xn1T_hi[:, c, :].bitcast(F32), ALU.subtract
                                        ).then_inc(S["xn1T_low"], 1)
                if x4:
                    top_two(*x4)
                if x0:
                    g, slot, rnd = x0
                    statistics(0, lambda j: embedded(j), S["ln1"], g * LN1_N, g)
                if x4:
                    gates(*x4)
                if x4:
                    g, slot, rnd = x4
                    at = g * POS_N
                    v.wait_ge(S["pos_ps"], g + 1)
                    wait(v, S["pos"], at)
                    carry = place[R, (slot - 1) % RING, GB, :]
                    v.tensor_tensor(place[R, slot, :, :],
                                    banks[4][R, 0:(GB + 1) * E8].rearrange("p (b e) -> p b e", e=E8),
                                    carry.unsqueeze(1).to_broadcast([TOK, GB + 1, E8]), ALU.add).then_inc(S["pos"], 1)
                if x0:
                    g, slot, rnd = x0
                    at = g * LN1_N
                    v.wait_ge(S["rstd1"], g * 2 + 2)
                    for j in range(GB):
                        v.scalar_tensor_tensor(out=y[R, j, :], in0=embedded(j), scalar=mv[R, 0, j, 0:1],
                                               in1=gamma_bc[R, :], op0=ALU.subtract, op1=ALU.mult).then_inc(S["ln1"], 1)
                    wait(v, h2_stored[slot], rnd * 16)
                    wait(v, S["xn2_ready"], (g - RING + 1) * GB)
                    for j in range(GB):
                        v.wait_ge(S["ln1"], at + 2 * GB + 1 + j)
                        v.scalar_tensor_tensor(out=h[R, slot, j, :], in0=y[R, j, :], scalar=rstd[R, 0, j:j + 1],
                                               in1=beta_bc[R, :], op0=ALU.mult, op1=ALU.add).then_inc(S["ln1"], 1)
                if x0:
                    g, slot, rnd = x0
                    statistics(1, lambda j: h[R, slot, j, :], S["ln1"], g * LN1_N + 4 * GB, g)
                if x4:
                    g, slot, rnd = x4
                    at = g * POS_N
                    v.wait_ge(S["pos"], at + 1)
                    v.tensor_tensor(placed[R, :, :, :], onehot[R, :, :, :],
                                    place[R, slot, 0:GB, :].unsqueeze(2).to_broadcast([TOK, GB, TOPK, E8]),
                                    ALU.mult).then_inc(S["pos"], 1)
                    v.wait_ge(S["pos"], at + 2)
                    v.tensor_reduce(rowf[R, :, :], placed[R, :, :, :], AX_X, ALU.add).then_inc(S["pos"], 1)
                    v.wait_ge(S["pos"], at + 3)
                    wait(v, scattered[slot], rnd * (16 * GB * TOPK))
                    v.tensor_copy(row_i[R, slot, :, :], rowf[R, :, :]).then_inc(S["pos"], 1)
                if x2:
                    g, slot, rnd = x2
                    v.wait_ge(S["probs_ready"], g * GB + GB)
                    v.reciprocal(rinv[R, :], rowsum[R, :]).then_inc(S["av"], 1)
                slot_it, rnd_it = slot_of(it, group_of)
                v.wait_ge(S["w_high"], it + 1)
                v.tensor_tensor(half_w[:, slot_it, 1, :], raw_w[:, slot_it, :], half_w[:, slot_it, 0, :].bitcast(F32),
                                ALU.subtract).then_inc(S["w_low"], 1)
                if x0:
                    g, slot, rnd = x0
                    v.wait_ge(S["rstd2"], g * 2 + 2)
                    v.scalar_tensor_tensor(out=nmr[R, 0, :], in0=mv[R, 1, :, 0], scalar=-1.0, in1=rstd[R, 1, :],
                                           op0=ALU.mult, op1=ALU.mult).then_inc(S["ln1"], 1)
                if x2:
                    g, slot, rnd = x2
                    at = g * AV_N
                    v.wait_ge(S["av"], at + 1)
                    for j in range(GB):
                        v.wait_ge(S["av_ps"], g * 2 + j // 2 + 1)
                        v.scalar_tensor_tensor(out=h[R, slot, j, :],
                                               in0=banks[1 + j // 2][R, (j % 2) * D:(j % 2 + 1) * D],
                                               scalar=rinv[R, j:j + 1], in1=h[R, slot, j, :],
                                               op0=ALU.mult, op1=ALU.add).then_inc(S["av"], 1)
                    statistics(2, lambda j: h[R, slot, j, :], S["av"], at + 1 + GB, g)
                if x3:
                    shifted_logits(*x3)

            def group(col):
                return col.unsqueeze(2).to_broadcast([TOK, GB, E8])

            def shifted_logits(g, slot, rnd):
                s = S["topk"]
                at = g * TOPK_N
                v.wait_ge(S["logits_ps"], g + 1)
                v.tensor_tensor(logits[R, :, 0:NE], banks[5][R, 0:GB * E8].rearrange("p (b e) -> p b e", e=E8)[:, :, 0:NE],
                                rb2_bc[R, :].unsqueeze(1).to_broadcast([TOK, GB, NE]), ALU.add).then_inc(s, 1)
                v.wait_ge(s, at + 1)
                v.tensor_reduce(lmax[R, :], logits[R, :, :], AX_X, ALU.max).then_inc(s, 1)
                v.wait_ge(s, at + 2)
                v.tensor_tensor(lshift[R, :, :], logits[R, :, :], group(lmax[R, :]), ALU.subtract).then_inc(s, 1)

            def top_two(g, slot, rnd):
                s = S["topk"]
                at = g * TOPK_N
                v.wait_ge(S["gate_exp"], g * 2 + 1)
                v.tensor_reduce(psums[R, :], pexp[R, :, :], AX_X, ALU.add).then_inc(s, 1)
                v.wait_ge(s, at + 4)
                v.reciprocal(pinv[R, :], psums[R, :]).then_inc(s, 1)
                v.wait_ge(s, at + 5)
                v.tensor_tensor(pn[R, :, :], pexp[R, :, :], group(pinv[R, :]), ALU.mult).then_inc(s, 1)
                wait_apart(v, s, at + 6, S["dve_passed"])
                for j in range(GB):
                    v.max(mx[R, j, :], pn[R, j, :]).then_inc(s, 1)
                for j in range(GB):
                    wait_apart(v, s, at + 7 + j, S["dve_passed"])
                    v.max_index(mxi[R, j, :], mx[R, j, :], pn[R, j, :]).then_inc(s, 1)
                v.tensor_tensor(gap[R, :], mx[R, :, 1], mx[R, :, 0], ALU.subtract).then_inc(s, 1)
                v.wait_ge(s, at + 14)
                v.tensor_copy(choice[R, :, :], mxi[R, :, 0:TOPK]).then_inc(s, 1)
                v.wait_ge(s, at + 16)
                v.tensor_tensor(onehot[R, :, :, :],
                                iota8[R, :].unsqueeze(1).unsqueeze(1).to_broadcast([TOK, GB, TOPK, E8]),
                                choice[R, :, :].unsqueeze(3).to_broadcast([TOK, GB, TOPK, E8]),
                                ALU.is_equal).then_inc(s, 1)
                v.wait_ge(s, at + 17)
                v.tensor_tensor(picked[R, :].rearrange("p (b e) -> p b e", e=E8), onehot[R, :, 0, :],
                                onehot[R, :, 1, :], ALU.add).then_inc(s, 1)

            def gates(g, slot, rnd):
                s = S["topk"]
                at = g * TOPK_N
                v.wait_ge(S["gate_exp"], g * 2 + 2)
                v.tensor_scalar(gden[R, :], gexp[R, :], 1.0, None, ALU.add).then_inc(s, 1)
                v.wait_ge(s, at + 19)
                v.reciprocal(gate2[R, :, 0], gden[R, :]).then_inc(s, 1)
                v.wait_ge(s, at + 20)
                v.tensor_tensor(gate2[R, :, 1], gexp[R, :], gate2[R, :, 0], ALU.mult).then_inc(s, 1)
                v.wait_ge(s, at + 21)
                v.tensor_tensor(gated[R, :, :, :], onehot[R, :, :, :],
                                gate2[R, :, :].unsqueeze(3).to_broadcast([TOK, GB, TOPK, E8]), ALU.mult).then_inc(s, 1)
                v.wait_ge(s, at + 22)
                v.tensor_tensor(rec[R, slot, :, D:D + E8], gated[R, :, 0, :], gated[R, :, 1, :], ALU.add).then_inc(s, 1)
                v.tensor_copy(rec[R, slot, :, D + E8:REC].bitcast(I32), tokid[R, :].unsqueeze(2)).then_inc(s, 1)
                v.tensor_scalar(tokid[R, :], tokid[R, :], float(GT), None, ALU.add).then_inc(s, 1)

            pipeline(v, step)

            s = S["table"]
            n = [0]

            def made(ins):
                ins.then_inc(s, 1)
                n[0] += 1
                v.wait_ge(s, n[0])

            ends = place[0:1, (G - 1) % RING, GB, :]
            v.wait_ge(S["pos"], G * POS_N)
            made(v.tensor_copy(pad_at[:], ends))
            made(v.tensor_tensor(t_nt[:], ends, t_base[:], ALU.subtract))
            made(v.tensor_scalar(t_i[:], t_nt[:], float(TILE - 1), None, ALU.add))
            made(v.tensor_scalar(t_ti[:], t_i[:], TILE.bit_length() - 1, None, ALU.arith_shift_right))
            made(v.tensor_copy(t_nt[:], t_ti[:]))
            made(v.tensor_tensor_scan(t_cum[:], t_nt[:], t_zero[:], 0.0, ALU.add, ALU.add))
            made(v.tensor_scalar(t_delta[:], t_nt[:], -float(TILE), float(REGION), ALU.mult, ALU.add))
            made(v.tensor_tensor(t_ge[:], t_iota[:].unsqueeze(2).to_broadcast([1, NT, E8]),
                                 t_cum[:].unsqueeze(1).to_broadcast([1, NT, E8]), ALU.is_ge))
            made(v.tensor_tensor(t_prod[:], t_ge[:], t_delta[:].unsqueeze(1).to_broadcast([1, NT, E8]), ALU.mult))
            made(v.tensor_reduce(t_row[:], t_prod[:, :, 0:NE], AX_X, ALU.add))
            made(v.scalar_tensor_tensor(out=t_row[:], in0=t_iota[:], scalar=float(TILE), in1=t_row[:],
                                        op0=ALU.mult, op1=ALU.add))
            made(v.tensor_scalar(row_tab[:], t_row[:], float(NE * REGION), None, ALU.min))
            made(v.tensor_reduce(t_exp[:], t_ge[:, :, 0:NE - 1], AX_X, ALU.add))
            v.tensor_copy(exp_tab[:], t_exp[:])
            v.tensor_scalar(t_load[:, 0:AHEAD], t_exp[:, 0:AHEAD], 0.0, None, ALU.not_equal)
            v.memset(t_load[:, AHEAD:SLOTS], 1.0)
            v.tensor_tensor(t_load[:, SLOTS:NT], t_exp[:, SLOTS:NT], t_exp[:, 0:NT - SLOTS], ALU.not_equal
                            ).then_inc(S["dve_const"], 1)
            v.wait_ge(S["dve_const"], 1)
            v.tensor_copy(load_tab[:], t_load[:]).then_inc(s, 1)

            def split_low(lo, val, hi, ready):
                v.tensor_tensor(lo, val, hi.bitcast(F32), ALU.subtract).then_inc(ready, 1)

            def rows_low(t, slot):
                wait(v, S["y_added"], (t - SLOTS + 1) * 16 * TB)
                v.wait_ge(S["txT_ps"], t * 2 + 2)
                v.tensor_copy(tail[:, slot, :, 0:E8], xg[:, slot, :, D:D + E8]).then_inc(S["tail_kept"], 1)
                v.tensor_copy(tail[:, slot, :, E8:].bitcast(I32), xg[:, slot, :, D + E8:REC].bitcast(I32)
                              ).then_inc(S["tail_kept"], 1)
                for c in range(DC):
                    v.wait_ge(S["tx_act"], t * 4 + 3 + c)
                    split_low(x_lo[:, c, :], xv[:, c, :], x_hi[:, c, :], S["tx_lo"])

            def split(t, val, hi, lo, made_by, s):
                for m in range(DC):
                    v.wait_ge(made_by, t * 2 + m + 1)
                    v.tensor_copy(hi[:, m, :], val[:, m, :]).then_inc(s, 1)
                    v.wait_ge(s, t * 4 + 2 * m + 1)
                    split_low(lo[:, m, :], val[:, m, :], hi[:, m, :], s)

            def tile_step(t, slot, rnd):
                inner = not isinstance(t, int)
                if inner or t < NT:
                    split(t, h1v, h1_hi, h1_lo, S["h1_v"], S["h1_split"])
                if inner or t + 1 < NT:
                    rows_low(t + 1, (slot + 1) % SLOTS)
                if inner or t >= 1:
                    p, ys = (slot - 1) % SLOTS, (slot - 1) % 2
                    at = (t - 1) * 4
                    wait(v, S["y_gated"], (t - 2) * TB)
                    v.wait_ge(w_loaded[p], (rnd - (1 if p == SLOTS - 1 else 0)) * 32 + 32)
                    v.tensor_tensor(gsel[:], tail[:, p, :, 0:E8],
                                    small[:, p, 2 * DC + D:SMALL].unsqueeze(1).to_broadcast([P, TB, E8]),
                                    ALU.mult).then_inc(S["y_dve"], 1)
                    v.wait_ge(S["y_dve"], at + 1)
                    v.tensor_reduce(gcol[:, ys, :], gsel[:], AX_X, ALU.add).then_inc(S["y_dve"], 1)
                    wait(v, S["y_added"], (t - 2) * 16 * TB)
                    for b in range(2):
                        v.wait_ge(S["y_ps"], (t - 1) * 2 + b + 1)
                        v.tensor_tensor(yo[:, ys, 2 * b:2 * b + 2, :],
                                        banks[6 + b][:].rearrange("p (b n) -> p b n", b=2),
                                        small[:, p, 2 * DC:2 * DC + D].unsqueeze(1).to_broadcast([P, 2, D]),
                                        ALU.add).then_inc(S["y_dve"], 1)
                if inner or t < NT:
                    split(t, h2v, h2_hi, h2_lo, S["h2_v"], S["h2_split"])

            rows_low(0, 0)
            tiles(v, tile_step)


def kernel(**inputs):
    import concourse.bacc as bacc
    from concourse.bass_utils import run_bass_kernel_spmd as run

    a = {k: np.asarray(v) for k, v in inputs.items()}

    def columns(v):
        return np.moveaxis(v.reshape(*v.shape[:-1], DC, P), -1, -2)

    onehot = np.broadcast_to(np.eye(NE, E8, dtype=np.float32)[:, None, :], (NE, P, E8))
    small = np.concatenate([columns(a["L0_ffn_expert_b1"]), columns(a["L0_ffn_expert_b2"]),
                            np.broadcast_to(a["L0_ffn_expert_b3"][:, None, :], (NE, P, D)), onehot], axis=2)
    arrays = {
        "x": a["x"].reshape(BATCH, ROWS_X, P),
        "tok_w": a["L0_tok_W"].T, "tok_b": a["L0_tok_b"][None], "tok_gamma": a["L0_tok_gamma"][None],
        "tok_beta": a["L0_tok_beta"][None],
        "wq": a["L0_attn_Wq"].T, "bq": columns(a["L0_attn_bq"]), "wk": a["L0_attn_Wk"].T,
        "bk": columns(a["L0_attn_bk"]), "wv": a["L0_attn_Wv"].T, "bv": a["L0_attn_bv"][None],
        "scale": a["L0_attn_scale"].reshape(1, 1),
        "rw1": a["L0_ffn_router_w1"], "rb1": a["L0_ffn_router_b1"][:, None], "rw2": a["L0_ffn_router_w2"],
        "rb2": a["L0_ffn_router_b2"][None],
        "eweights": np.stack([a[f"L0_ffn_expert_w{i}"] for i in (1, 2, 3)], axis=1).reshape(NCHUNK, P, D),
        "esmall": small,
    }
    nc = bacc.Bacc("TRN2", target_bir_lowering=False, num_devices=1)
    feeds, args = {}, []
    for name, v in arrays.items():
        v = np.ascontiguousarray(v)
        feeds[f"in_{name}"] = v
        args.append(nc.dram_tensor(f"in_{name}", v.shape, mybir.dt.from_np(v.dtype), kind="ExternalInput").ap())
    out = nc.dram_tensor("out", [NTOK + TILE, D], F32, kind="ExternalOutput").ap()
    audio_tower(nc, *args, out)
    r = run(nc, [feeds], core_ids=[0])
    return r.results[0]["out"][:NTOK].reshape(BATCH, TOK, D)
```
